# Optimizing a Trainium2 kernel written in Bass

```python
import numpy as np
import jax
import jax.numpy as jnp

def _softmax(x, axis=-1):
    return jax.nn.softmax(x, axis=axis)

def _gelu(x):
    return jax.nn.gelu(x, approximate=True)

def _silu(x):
    return jax.nn.silu(x)

def _sigmoid(x):
    return jax.nn.sigmoid(x)

def _layernorm(x, axis=-1, eps=1e-05):
    m = jnp.mean(x, axis=axis, keepdims=True)
    v = jnp.var(x, axis=axis, keepdims=True)
    return (x - m) / jnp.sqrt(v + eps)

def _scatter_add(tgt, idx, src, axis=0):
    return tgt.at[idx].add(src)

def _segment_sum(src, seg, n):
    return jax.ops.segment_sum(src, seg, n)
kernel_name = 'mk_recurrent_d4_jaxref_r8_28fdd6'

def setup_inputs(seed: int=0):
    np.random.seed(seed)
    _w = jnp.asarray

    def _L0_attn_setup():
        import jax, jax.numpy as jnp
        import numpy as np
        DIM = 128
        HIDDEN = 192
        K = 4
        ALPHA_LOG_SCALE = -8.0

        def _causal_depthwise_conv(x, w, b):
            T = x.shape[1]
            xp = jnp.pad(x, ((0, 0), (K - 1, 0), (0, 0)))
            y = b
            for k in range(K):
                y = y + w[:, k] * xp[:, k:k + T, :]
            return y

        def _rglru_scan(alpha, xs):

            def combine(c1, c2):
                a1, x1 = c1
                a2, x2 = c2
                return (a1 * a2, a2 * x1 + x2)
            _, h = jax.lax.associative_scan(combine, (alpha, xs), axis=1)
            return h
        key = jax.random.key(seed)
        ks = jax.random.split(key, 7)
        x = jax.random.normal(ks[0], (8, 256, DIM), dtype=jnp.float32)
        W_in = jax.random.normal(ks[1], (2 * HIDDEN, DIM), dtype=jnp.float32) * DIM ** (-0.5)
        conv_w = jax.random.normal(ks[2], (HIDDEN, K), dtype=jnp.float32) * (1.0 / K) ** 0.5
        conv_b = jax.random.normal(ks[3], (HIDDEN,), dtype=jnp.float32) * 0.02
        W_gates = jax.random.normal(ks[4], (2 * HIDDEN, HIDDEN), dtype=jnp.float32) * HIDDEN ** (-0.5)
        b_gates = jnp.zeros((2 * HIDDEN,), dtype=jnp.float32)
        forget_base = jnp.linspace(-4.323, -9.0, HIDDEN, dtype=jnp.float32)
        W_out = jax.random.normal(ks[5], (DIM, HIDDEN), dtype=jnp.float32) * HIDDEN ** (-0.5)
        return {'x': x, 'W_in': W_in, 'conv_w': conv_w, 'conv_b': conv_b, 'W_gates': W_gates, 'b_gates': b_gates, 'forget_base': forget_base, 'W_out': W_out}
    _L0_attn_in = _L0_attn_setup()

    def _L0_ffn_setup():
        import jax, jax.numpy as jnp
        import numpy as np
        R = 64
        key = jax.random.key(seed)
        k1, k2, k3 = jax.random.split(key, 3)
        B, S, D_IN, D_OUT = (8, 512, 128, 128)
        x = jax.random.normal(k1, (B, S, D_IN), dtype=jnp.float32)
        weight = jax.random.normal(k2, (D_OUT, D_IN), dtype=jnp.float32) * (1.0 / np.sqrt(D_IN))
        disha = jax.random.normal(k3, (R, D_OUT), dtype=jnp.float32) * 0.01
        return {'x': x, 'weight': weight, 'disha': disha}
    _L0_ffn_in = _L0_ffn_setup()

    def _L1_attn_setup():
        import jax, jax.numpy as jnp
        import numpy as np
        L, D, HS, E, ED, FE = (2, 128, 64, 32, 64, 3)
        H = D // HS
        B, T = (4, 256)
        EPS = 1e-05

        def _ln(x, w):
            mu = x.mean(-1, keepdims=True)
            var = ((x - mu) ** 2).mean(-1, keepdims=True)
            return (x - mu) / jnp.sqrt(var + EPS) * w

        def _shift(x):
            return jnp.concatenate([jnp.zeros_like(x[:, :1]), x[:, :-1]], axis=1)

        def _wkv(r, k, v, w, u):

            def step(state, inp):
                rt, kt, vt, wt = inp
                kv = kt[..., :, None] * vt[..., None, :]
                out = jnp.einsum('bhk,bhkv->bhv', rt, state + u[None, :, :, None] * kv)
                return (state * wt[..., None] + kv, out)
            init = jnp.zeros((r.shape[0], r.shape[1], r.shape[3], v.shape[3]), r.dtype)
            xs = tuple((jnp.moveaxis(a, 2, 0) for a in (r, k, v, w)))
            _, outs = jax.lax.scan(step, init, xs)
            return jnp.moveaxis(outs, 0, 2)

        def _time_mix(x, p):
            b, t, d = x.shape
            sx = _shift(x) - x
            xxx = x + sx * p['x_maa']
            mix = jnp.tanh(xxx @ p['tm_w1']).reshape(b * t, 5, E)
            mix = jnp.einsum('nfe,fed->fnd', mix, p['tm_w2']).reshape(5, b, t, d)
            mw, mk, mv, mr, mg = mix
            wx = x + sx * (p['w_maa'] + mw)
            kx = x + sx * (p['k_maa'] + mk)
            vx = x + sx * (p['v_maa'] + mv)
            rx = x + sx * (p['r_maa'] + mr)
            gx = x + sx * (p['g_maa'] + mg)
            r = jax.nn.sigmoid(rx @ p['Wr'])
            k = kx @ p['Wk']
            v = vx @ p['Wv']
            g = jax.nn.silu(gx @ p['Wg'])
            w = jnp.tanh(wx @ p['td_w1']) @ p['td_w2']
            w = jnp.exp(-jnp.exp(p['time_decay'][None, :, None, :] + w.reshape(b, t, H, HS).transpose(0, 2, 1, 3)))
            r4 = r.reshape(b, t, H, HS).transpose(0, 2, 1, 3)
            k4 = k.reshape(b, t, H, HS).transpose(0, 2, 1, 3)
            v4 = v.reshape(b, t, H, HS).transpose(0, 2, 1, 3)
            out = _wkv(r4, k4, v4, w, p['time_first']).transpose(0, 2, 1, 3).reshape(b * t, H, HS)
            mu = out.mean(-1, keepdims=True)
            var = ((out - mu) ** 2).mean(-1, keepdims=True)
            out = ((out - mu) / jnp.sqrt(var + EPS)).reshape(b * t, d) * p['gn_w'] + p['gn_b']
            return out.reshape(b, t, d) * g @ p['Wo']

        def _channel_mix(x, p):
            sx = _shift(x) - x
            k = jnp.square(jax.nn.relu((x + sx * p['ck_maa']) @ p['cWk']))
            return jax.nn.sigmoid((x + sx * p['cr_maa']) @ p['cWr']) * (k @ p['cWv'])
        PER_LAYER = ['ln1_w', 'ln2_w', 'x_maa', 'w_maa', 'k_maa', 'v_maa', 'r_maa', 'g_maa', 'tm_w1', 'tm_w2', 'td_w1', 'td_w2', 'time_decay', 'time_first', 'Wr', 'Wk', 'Wv', 'Wo', 'Wg', 'gn_w', 'gn_b', 'ck_maa', 'cr_maa', 'cWk', 'cWv', 'cWr']

        def _forward(x, params):
            for i in range(L):
                p = {n: params[n][i] for n in PER_LAYER}
                x = x + _time_mix(_ln(x, p['ln1_w']), p)
                x = x + _channel_mix(_ln(x, p['ln2_w']), p)
            return _ln(x, params['ln_out_w'])
        key = jax.random.key(seed)
        ks = jax.random.split(key, 20)

        def nrm(k, shape, s=0.02):
            return jax.random.normal(k, shape, dtype=jnp.float32) * s

        def uni(k, shape):
            return jax.random.uniform(k, shape, dtype=jnp.float32)
        return dict(x=jax.random.normal(ks[0], (B, T, D), dtype=jnp.float32), ln1_w=jnp.ones((L, D), jnp.float32), ln2_w=jnp.ones((L, D), jnp.float32), x_maa=uni(ks[1], (L, D)), w_maa=uni(ks[2], (L, D)), k_maa=uni(ks[3], (L, D)), v_maa=uni(ks[4], (L, D)), r_maa=uni(ks[5], (L, D)), g_maa=uni(ks[6], (L, D)), tm_w1=nrm(ks[7], (L, D, 5 * E)), tm_w2=nrm(ks[8], (L, 5, E, D)), td_w1=nrm(ks[9], (L, D, ED)), td_w2=nrm(ks[10], (L, ED, D)), time_decay=jax.random.uniform(ks[11], (L, H, HS), jnp.float32, -6.0, -1.0), time_first=nrm(ks[12], (L, H, HS), 0.3), Wr=nrm(ks[13], (L, D, D)), Wk=nrm(ks[14], (L, D, D)), Wv=nrm(ks[15], (L, D, D)), Wo=nrm(ks[16], (L, D, D)), Wg=nrm(ks[17], (L, D, D)), gn_w=jnp.ones((L, D), jnp.float32), gn_b=jnp.zeros((L, D), jnp.float32), ck_maa=uni(ks[18], (L, D)), cr_maa=uni(ks[19], (L, D)), cWk=nrm(jax.random.fold_in(key, 100), (L, D, FE * D)), cWv=nrm(jax.random.fold_in(key, 101), (L, FE * D, D)), cWr=nrm(jax.random.fold_in(key, 102), (L, D, D)), ln_out_w=jnp.ones((D,), jnp.float32))
    _L1_attn_in = _L1_attn_setup()

    def _L1_ffn_setup():
        import jax, jax.numpy as jnp
        import numpy as np
        DIM = 128
        DEPTH = 6
        HEADS = 16
        DIM_HEAD = 64
        WINDOW = 32
        INNER = HEADS * DIM_HEAD
        DIM_INNER = int(DIM * 4 * 2 / 3)
        QK_SCALE = 8.0

        def shift_tokens(t):
            a, s = jnp.split(t, 2, -1)
            s = jnp.pad(s, ((0, 0), (1, 0), (0, 0)))[:, :-1]
            return jnp.concatenate([a, s], -1)

        def l2norm(t):
            return t / jnp.maximum(jnp.linalg.norm(t, axis=-1, keepdims=True), 1e-12)

        def rotate_half(x):
            x1, x2 = jnp.split(x, 2, -1)
            return jnp.concatenate([-x2, x1], -1)

        def rotary_tables(n):
            half = jnp.arange(0, DIM_HEAD, 2, dtype=jnp.float32)
            inv_freq = 1.0 / 10000.0 ** (half / DIM_HEAD)
            t = jnp.arange(n, dtype=jnp.float32)
            freqs = t[:, None] * inv_freq[None, :]
            freqs = jnp.concatenate([freqs, freqs], -1)
            base_scale = (half + 0.4 * DIM_HEAD) / (1.4 * DIM_HEAD)
            power = (t - n // 2) / (WINDOW // 2)
            scale = base_scale[None, :] ** power[:, None]
            scale = jnp.concatenate([scale, scale], -1)
            return (freqs, scale)

        def local_attention(q, k, v):
            b, h, n, d = q.shape
            w = WINDOW
            nw = n // w
            bq = q.reshape(b, h, nw, w, d)
            bk = k.reshape(b, h, nw, w, d)
            bv = v.reshape(b, h, nw, w, d)

            def look(t):
                p = jnp.pad(t, ((0, 0), (0, 0), (1, 0), (0, 0), (0, 0)))
                return jnp.concatenate([p[:, :, :nw], p[:, :, 1:]], axis=3)
            bk2, bv2 = (look(bk), look(bv))
            seq = jnp.arange(n).reshape(nw, w)
            seq_p = jnp.pad(seq, ((1, 0), (0, 0)), constant_values=-1)
            jt = jnp.concatenate([seq_p[:nw], seq_p[1:]], axis=1)
            it = seq[:, :, None]
            jb = jt[:, None, :]
            mask = (it < jb) | (it > jb + w) | (jb == -1)
            sim = jnp.einsum('bhwie,bhwje->bhwij', bq, bk2) * QK_SCALE
            sim = jnp.where(mask, -jnp.finfo(sim.dtype).max, sim)
            attn = jax.nn.softmax(sim, -1)
            out = jnp.einsum('bhwij,bhwje->bhwie', attn, bv2)
            return out.reshape(b, h, n, d)

        def attn_layer(x, Wqkv, qs, ksc, Wo):
            b, n, _ = x.shape
            qkv = x @ Wqkv
            q, k, v = jnp.split(qkv, 3, -1)
            sh = lambda t: t.reshape(b, n, HEADS, DIM_HEAD).transpose(0, 2, 1, 3)
            q, k, v = (sh(q), sh(k), sh(v))
            q = l2norm(q) * qs
            k = l2norm(k) * ksc
            freqs, scale = rotary_tables(n)
            cos, sin = (jnp.cos(freqs), jnp.sin(freqs))
            q = q * cos * scale + rotate_half(q) * sin * scale
            inv = 1.0 / scale
            k = k * cos * inv + rotate_half(k) * sin * inv
            out = local_attention(q, k, v)
            out = out.transpose(0, 2, 1, 3).reshape(b, n, INNER)
            return out @ Wo

        def ffn_layer(x, g, bln, W1, b1, W2, b2):
            mu = x.mean(-1, keepdims=True)
            var = ((x - mu) ** 2).mean(-1, keepdims=True)
            xn = (x - mu) / jnp.sqrt(var + 1e-05) * g + bln
            hg = xn @ W1 + b1
            a, gate = jnp.split(hg, 2, -1)
            return a * jax.nn.gelu(gate, approximate=False) @ W2 + b2
        key = jax.random.key(seed)
        ks = jax.random.split(key, 8)
        B, N = (2, 256)
        init = lambda k, shape: jax.random.normal(k, shape, jnp.float32) * 0.02
        return {'x': jax.random.normal(ks[0], (B, N, DIM), jnp.float32), 'Wqkv': init(ks[1], (DEPTH, DIM, 3 * INNER)), 'q_scale': jnp.ones((DEPTH, DIM_HEAD), jnp.float32), 'k_scale': jnp.ones((DEPTH, DIM_HEAD), jnp.float32), 'Wo': init(ks[2], (DEPTH, INNER, DIM)), 'ln_g': jnp.ones((DEPTH, DIM), jnp.float32), 'ln_b': jnp.zeros((DEPTH, DIM), jnp.float32), 'W1': init(ks[3], (DEPTH, DIM, 2 * DIM_INNER)), 'b1': jnp.zeros((DEPTH, 2 * DIM_INNER), jnp.float32), 'W2': init(ks[4], (DEPTH, DIM_INNER, DIM)), 'b2': jnp.zeros((DEPTH, DIM), jnp.float32)}
    _L1_ffn_in = _L1_ffn_setup()

    def _L2_attn_setup():
        import jax, jax.numpy as jnp
        import numpy as np
        import math
        NHEAD = 16
        FACTOR = 5
        key = jax.random.key(seed)
        ks = jax.random.split(key, 10)
        B, L, Dm = (2, 256, 128)
        x = jax.random.normal(ks[0], (B, L, Dm), dtype=jnp.float32)
        w = lambda k: jax.random.normal(k, (Dm, Dm), dtype=jnp.float32) * 0.02
        b = lambda k: jax.random.normal(k, (Dm,), dtype=jnp.float32) * 0.02
        return {'x': x, 'Wq': w(ks[1]), 'bq': b(ks[2]), 'Wk': w(ks[3]), 'bk': b(ks[4]), 'Wv': w(ks[5]), 'bv': b(ks[6]), 'Wo': w(ks[7]), 'bo': b(ks[8])}
    _L2_attn_in = _L2_attn_setup()

    def _L2_ffn_setup():
        import jax, jax.numpy as jnp
        import numpy as np
        TOP_K = 4
        N_GROUP = 4
        TOPK_GROUP = 2
        ROUTED_SCALING = 1.0

        def _route(x_flat, gate_weight, e_bias):
            T = x_flat.shape[0]
            E = gate_weight.shape[0]
            logits = jnp.einsum('th,eh->te', x_flat, gate_weight)
            scores = jax.nn.sigmoid(logits)
            scores_for_choice = scores + e_bias[None, :]
            grp = scores_for_choice.reshape(T, N_GROUP, E // N_GROUP)
            top2, _ = jax.lax.top_k(grp, 2)
            group_scores = top2.sum(axis=-1)
            _, group_idx = jax.lax.top_k(group_scores, TOPK_GROUP)
            group_mask = jax.nn.one_hot(group_idx, N_GROUP, dtype=scores.dtype).sum(axis=1)
            score_mask = jnp.repeat(group_mask, E // N_GROUP, axis=1)
            tmp_scores = jnp.where(score_mask > 0, scores_for_choice, 0.0)
            _, topk_idx = jax.lax.top_k(tmp_scores, TOP_K)
            topk_weight = jnp.take_along_axis(scores, topk_idx, axis=1)
            denom = topk_weight.sum(axis=-1, keepdims=True) + 1e-20
            topk_weight = topk_weight / denom * ROUTED_SCALING
            return (topk_idx, topk_weight)
        key = jax.random.key(seed)
        k1, k2, k3, k4, k5 = jax.random.split(key, 5)
        B, S, H, I, E = (1, 256, 128, 64, 16)
        hidden_states = jax.random.normal(k1, (B, S, H), dtype=jnp.float32)
        gate_weight = jax.random.normal(k2, (E, H), dtype=jnp.float32) * (1.0 / np.sqrt(H))
        e_bias = jnp.zeros((E,), dtype=jnp.float32)
        gate_proj = jax.random.normal(k3, (E, I, H), dtype=jnp.float32) * 0.02
        up_proj = jax.random.normal(k4, (E, I, H), dtype=jnp.float32) * 0.02
        down_proj = jax.random.normal(k5, (E, H, I), dtype=jnp.float32) * 0.02
        return {'hidden_states': hidden_states, 'gate_weight': gate_weight, 'e_bias': e_bias, 'gate_proj': gate_proj, 'up_proj': up_proj, 'down_proj': down_proj}
    _L2_ffn_in = _L2_ffn_setup()

    def _L3_attn_setup():
        import jax, jax.numpy as jnp
        import numpy as np
        B, S, D, L = (4, 256, 128, 4)

        def _retention(x, wkqv):
            d = x.shape[-1]
            k, q, v = jnp.split(x @ wkqv, 3, axis=-1)
            qkt = jnp.einsum('bid,bjd->bij', q, k) / jnp.sqrt(jnp.float32(d))
            s = x.shape[1]
            row_norm = 1.0 + jnp.sqrt(jnp.arange(s, dtype=x.dtype))[None, :, None]
            r = jnp.tril(qkt) / row_norm
            denom = jnp.clip(jnp.abs(r.sum(-1, keepdims=True)), 1.0, None)
            r = r / denom
            return jnp.einsum('bij,bjd->bid', r, v)

        def _groupnorm1(y, g, b, eps=1e-05):
            mu = y.mean(axis=(1, 2), keepdims=True)
            var = y.var(axis=(1, 2), keepdims=True)
            return (y - mu) / jnp.sqrt(var + eps) * g + b

        def _layernorm(y, g, b, eps=1e-05):
            mu = y.mean(-1, keepdims=True)
            var = y.var(-1, keepdims=True)
            return (y - mu) / jnp.sqrt(var + eps) * g + b
        key = jax.random.key(seed)
        ks = jax.random.split(key, 6)
        w = lambda k, shape: jax.random.normal(k, shape, jnp.float32) * 0.02
        return {'x': jax.random.normal(ks[0], (B, S, D), jnp.float32), 'Wkqv': w(ks[1], (L, D, 3 * D)), 'Wm1': w(ks[2], (L, D, 2 * D)), 'bm1': jnp.zeros((L, 2 * D), jnp.float32), 'Wm2': w(ks[3], (L, D, D)), 'bm2': jnp.zeros((L, D), jnp.float32), 'gn_g': jnp.ones((L, D), jnp.float32), 'gn_b': jnp.zeros((L, D), jnp.float32), 'Wf1': w(ks[4], (L, D, 2 * D)), 'bf1': jnp.zeros((L, 2 * D), jnp.float32), 'Wf2': w(ks[5], (L, 2 * D, D)), 'bf2': jnp.zeros((L, D), jnp.float32), 'ln_g': jnp.ones((L, D), jnp.float32), 'ln_b': jnp.zeros((L, D), jnp.float32)}
    _L3_attn_in = _L3_attn_setup()

    def _L3_ffn_setup():
        import jax, jax.numpy as jnp
        import numpy as np
        B, T, D, E, H = (4, 256, 128, 4, 8)
        EPS = 1e-05

        def _uniform(k, shape, bound):
            return jax.random.uniform(k, shape, jnp.float32, -bound, bound)

        def _layernorm(x, w, b):
            mu = jnp.mean(x, axis=-1, keepdims=True)
            var = jnp.mean(jnp.square(x - mu), axis=-1, keepdims=True)
            return (x - mu) * jax.lax.rsqrt(var + EPS) * w + b
        key = jax.random.key(seed)
        ks = jax.random.split(key, 12)
        wb = np.sqrt(6.0 / D) / np.sqrt(6.0)
        wb = 1.0 / np.sqrt(D)
        return {'x': jax.random.normal(ks[0], (B, T, D), jnp.float32), 'router_prob': jax.random.uniform(ks[1], (B, T, E), jnp.float32), 'norm_w': jnp.ones((D,), jnp.float32), 'norm_b': jnp.zeros((D,), jnp.float32), 'q_w': _uniform(ks[2], (D, D), wb), 'q_b': _uniform(ks[3], (D,), wb), 'k_w': _uniform(ks[4], (D, D), wb), 'k_b': _uniform(ks[5], (D,), wb), 'v_w': _uniform(ks[6], (D, D), wb), 'v_b': _uniform(ks[7], (D,), wb), 'o_w': _uniform(ks[8], (D, D), wb), 'o_b': _uniform(ks[9], (D,), wb)}
    _L3_ffn_in = _L3_ffn_setup()
    _d = {'L0_attn_x': _L0_attn_in['x'], 'L0_attn_W_in': _L0_attn_in['W_in'], 'L0_attn_conv_w': _L0_attn_in['conv_w'], 'L0_attn_conv_b': _L0_attn_in['conv_b'], 'L0_attn_W_gates': _L0_attn_in['W_gates'], 'L0_attn_b_gates': _L0_attn_in['b_gates'], 'L0_attn_forget_base': _L0_attn_in['forget_base'], 'L0_attn_W_out': _L0_attn_in['W_out'], 'L0_ffn_weight': _L0_ffn_in['weight'], 'L0_ffn_disha': _L0_ffn_in['disha'], 'L1_attn_ln1_w': _L1_attn_in['ln1_w'], 'L1_attn_ln2_w': _L1_attn_in['ln2_w'], 'L1_attn_x_maa': _L1_attn_in['x_maa'], 'L1_attn_w_maa': _L1_attn_in['w_maa'], 'L1_attn_k_maa': _L1_attn_in['k_maa'], 'L1_attn_v_maa': _L1_attn_in['v_maa'], 'L1_attn_r_maa': _L1_attn_in['r_maa'], 'L1_attn_g_maa': _L1_attn_in['g_maa'], 'L1_attn_tm_w1': _L1_attn_in['tm_w1'], 'L1_attn_tm_w2': _L1_attn_in['tm_w2'], 'L1_attn_td_w1': _L1_attn_in['td_w1'], 'L1_attn_td_w2': _L1_attn_in['td_w2'], 'L1_attn_time_decay': _L1_attn_in['time_decay'], 'L1_attn_time_first': _L1_attn_in['time_first'], 'L1_attn_Wr': _L1_attn_in['Wr'], 'L1_attn_Wk': _L1_attn_in['Wk'], 'L1_attn_Wv': _L1_attn_in['Wv'], 'L1_attn_Wo': _L1_attn_in['Wo'], 'L1_attn_Wg': _L1_attn_in['Wg'], 'L1_attn_gn_w': _L1_attn_in['gn_w'], 'L1_attn_gn_b': _L1_attn_in['gn_b'], 'L1_attn_ck_maa': _L1_attn_in['ck_maa'], 'L1_attn_cr_maa': _L1_attn_in['cr_maa'], 'L1_attn_cWk': _L1_attn_in['cWk'], 'L1_attn_cWv': _L1_attn_in['cWv'], 'L1_attn_cWr': _L1_attn_in['cWr'], 'L1_attn_ln_out_w': _L1_attn_in['ln_out_w'], 'L1_ffn_Wqkv': _L1_ffn_in['Wqkv'], 'L1_ffn_q_scale': _L1_ffn_in['q_scale'], 'L1_ffn_k_scale': _L1_ffn_in['k_scale'], 'L1_ffn_Wo': _L1_ffn_in['Wo'], 'L1_ffn_ln_g': _L1_ffn_in['ln_g'], 'L1_ffn_ln_b': _L1_ffn_in['ln_b'], 'L1_ffn_W1': _L1_ffn_in['W1'], 'L1_ffn_b1': _L1_ffn_in['b1'], 'L1_ffn_W2': _L1_ffn_in['W2'], 'L1_ffn_b2': _L1_ffn_in['b2'], 'L2_attn_Wq': _L2_attn_in['Wq'], 'L2_attn_bq': _L2_attn_in['bq'], 'L2_attn_Wk': _L2_attn_in['Wk'], 'L2_attn_bk': _L2_attn_in['bk'], 'L2_attn_Wv': _L2_attn_in['Wv'], 'L2_attn_bv': _L2_attn_in['bv'], 'L2_attn_Wo': _L2_attn_in['Wo'], 'L2_attn_bo': _L2_attn_in['bo'], 'L2_ffn_gate_weight': _L2_ffn_in['gate_weight'], 'L2_ffn_e_bias': _L2_ffn_in['e_bias'], 'L2_ffn_gate_proj': _L2_ffn_in['gate_proj'], 'L2_ffn_up_proj': _L2_ffn_in['up_proj'], 'L2_ffn_down_proj': _L2_ffn_in['down_proj'], 'L3_attn_Wkqv': _L3_attn_in['Wkqv'], 'L3_attn_Wm1': _L3_attn_in['Wm1'], 'L3_attn_bm1': _L3_attn_in['bm1'], 'L3_attn_Wm2': _L3_attn_in['Wm2'], 'L3_attn_bm2': _L3_attn_in['bm2'], 'L3_attn_gn_g': _L3_attn_in['gn_g'], 'L3_attn_gn_b': _L3_attn_in['gn_b'], 'L3_attn_Wf1': _L3_attn_in['Wf1'], 'L3_attn_bf1': _L3_attn_in['bf1'], 'L3_attn_Wf2': _L3_attn_in['Wf2'], 'L3_attn_bf2': _L3_attn_in['bf2'], 'L3_attn_ln_g': _L3_attn_in['ln_g'], 'L3_attn_ln_b': _L3_attn_in['ln_b'], 'L3_ffn_router_prob': _L3_ffn_in['router_prob'], 'L3_ffn_norm_w': _L3_ffn_in['norm_w'], 'L3_ffn_norm_b': _L3_ffn_in['norm_b'], 'L3_ffn_q_w': _L3_ffn_in['q_w'], 'L3_ffn_q_b': _L3_ffn_in['q_b'], 'L3_ffn_k_w': _L3_ffn_in['k_w'], 'L3_ffn_k_b': _L3_ffn_in['k_b'], 'L3_ffn_v_w': _L3_ffn_in['v_w'], 'L3_ffn_v_b': _L3_ffn_in['v_b'], 'L3_ffn_o_w': _L3_ffn_in['o_w'], 'L3_ffn_o_b': _L3_ffn_in['o_b']}
    _x0 = _d['L0_attn_x']
    _d['L0_attn_x'] = jax.random.normal(jax.random.fold_in(jax.random.key(seed), 1), (4, 512, 128), dtype=_x0.dtype)
    del _x0
    return _d

def reference(L0_attn_x, L0_attn_W_in, L0_attn_conv_w, L0_attn_conv_b, L0_attn_W_gates, L0_attn_b_gates, L0_attn_forget_base, L0_attn_W_out, L0_ffn_weight, L0_ffn_disha, L1_attn_ln1_w, L1_attn_ln2_w, L1_attn_x_maa, L1_attn_w_maa, L1_attn_k_maa, L1_attn_v_maa, L1_attn_r_maa, L1_attn_g_maa, L1_attn_tm_w1, L1_attn_tm_w2, L1_attn_td_w1, L1_attn_td_w2, L1_attn_time_decay, L1_attn_time_first, L1_attn_Wr, L1_attn_Wk, L1_attn_Wv, L1_attn_Wo, L1_attn_Wg, L1_attn_gn_w, L1_attn_gn_b, L1_attn_ck_maa, L1_attn_cr_maa, L1_attn_cWk, L1_attn_cWv, L1_attn_cWr, L1_attn_ln_out_w, L1_ffn_Wqkv, L1_ffn_q_scale, L1_ffn_k_scale, L1_ffn_Wo, L1_ffn_ln_g, L1_ffn_ln_b, L1_ffn_W1, L1_ffn_b1, L1_ffn_W2, L1_ffn_b2, L2_attn_Wq, L2_attn_bq, L2_attn_Wk, L2_attn_bk, L2_attn_Wv, L2_attn_bv, L2_attn_Wo, L2_attn_bo, L2_ffn_gate_weight, L2_ffn_e_bias, L2_ffn_gate_proj, L2_ffn_up_proj, L2_ffn_down_proj, L3_attn_Wkqv, L3_attn_Wm1, L3_attn_bm1, L3_attn_Wm2, L3_attn_bm2, L3_attn_gn_g, L3_attn_gn_b, L3_attn_Wf1, L3_attn_bf1, L3_attn_Wf2, L3_attn_bf2, L3_attn_ln_g, L3_attn_ln_b, L3_ffn_router_prob, L3_ffn_norm_w, L3_ffn_norm_b, L3_ffn_q_w, L3_ffn_q_b, L3_ffn_k_w, L3_ffn_k_b, L3_ffn_v_w, L3_ffn_v_b, L3_ffn_o_w, L3_ffn_o_b):

    def _L0_attn_ref(x, W_in, conv_w, conv_b, W_gates, b_gates, forget_base, W_out):
        import jax, jax.numpy as jnp
        import numpy as np
        DIM = 128
        HIDDEN = 192
        K = 4
        ALPHA_LOG_SCALE = -8.0

        def _causal_depthwise_conv(x, w, b):
            T = x.shape[1]
            xp = jnp.pad(x, ((0, 0), (K - 1, 0), (0, 0)))
            y = b
            for k in range(K):
                y = y + w[:, k] * xp[:, k:k + T, :]
            return y

        def _rglru_scan(alpha, xs):

            def combine(c1, c2):
                a1, x1 = c1
                a2, x2 = c2
                return (a1 * a2, a2 * x1 + x2)
            _, h = jax.lax.associative_scan(combine, (alpha, xs), axis=1)
            return h
        u = jnp.einsum('ntc,hc->nth', x, W_in)
        gate, xh = jnp.split(u, 2, axis=-1)
        xh = _causal_depthwise_conv(xh, conv_w, conv_b)
        g = jnp.einsum('nth,gh->ntg', xh, W_gates) + b_gates
        forget, inp = jnp.split(g, 2, axis=-1)
        log_alpha = ALPHA_LOG_SCALE * jax.nn.softplus(forget_base) * jax.nn.sigmoid(forget)
        alpha = jnp.exp(log_alpha)
        beta = jnp.sqrt(1.0 - alpha ** 2 + 1e-06)
        xs = beta * jax.nn.sigmoid(inp) * xh
        h = _rglru_scan(alpha, xs)
        out = jnp.einsum('nth,dh->ntd', jax.nn.gelu(gate, approximate=False) * h, W_out)
        return out

    def _L0_ffn_ref(x, weight, disha):
        import jax, jax.numpy as jnp
        import numpy as np
        R = 64
        result = jnp.einsum('bsd,od->bso', x, weight)
        r = disha.shape[0]
        pooled = x.reshape(*x.shape[:-1], x.shape[-1] // r, r).sum(axis=-2)
        return result + pooled @ disha

    def _L1_attn_ref(x, ln1_w, ln2_w, x_maa, w_maa, k_maa, v_maa, r_maa, g_maa, tm_w1, tm_w2, td_w1, td_w2, time_decay, time_first, Wr, Wk, Wv, Wo, Wg, gn_w, gn_b, ck_maa, cr_maa, cWk, cWv, cWr, ln_out_w):
        import jax, jax.numpy as jnp
        import numpy as np
        L, D, HS, E, ED, FE = (2, 128, 64, 32, 64, 3)
        H = D // HS
        B, T = (4, 256)
        EPS = 1e-05

        def _ln(x, w):
            mu = x.mean(-1, keepdims=True)
            var = ((x - mu) ** 2).mean(-1, keepdims=True)
            return (x - mu) / jnp.sqrt(var + EPS) * w

        def _shift(x):
            return jnp.concatenate([jnp.zeros_like(x[:, :1]), x[:, :-1]], axis=1)

        def _wkv(r, k, v, w, u):

            def step(state, inp):
                rt, kt, vt, wt = inp
                kv = kt[..., :, None] * vt[..., None, :]
                out = jnp.einsum('bhk,bhkv->bhv', rt, state + u[None, :, :, None] * kv)
                return (state * wt[..., None] + kv, out)
            init = jnp.zeros((r.shape[0], r.shape[1], r.shape[3], v.shape[3]), r.dtype)
            xs = tuple((jnp.moveaxis(a, 2, 0) for a in (r, k, v, w)))
            _, outs = jax.lax.scan(step, init, xs)
            return jnp.moveaxis(outs, 0, 2)

        def _time_mix(x, p):
            b, t, d = x.shape
            sx = _shift(x) - x
            xxx = x + sx * p['x_maa']
            mix = jnp.tanh(xxx @ p['tm_w1']).reshape(b * t, 5, E)
            mix = jnp.einsum('nfe,fed->fnd', mix, p['tm_w2']).reshape(5, b, t, d)
            mw, mk, mv, mr, mg = mix
            wx = x + sx * (p['w_maa'] + mw)
            kx = x + sx * (p['k_maa'] + mk)
            vx = x + sx * (p['v_maa'] + mv)
            rx = x + sx * (p['r_maa'] + mr)
            gx = x + sx * (p['g_maa'] + mg)
            r = jax.nn.sigmoid(rx @ p['Wr'])
            k = kx @ p['Wk']
            v = vx @ p['Wv']
            g = jax.nn.silu(gx @ p['Wg'])
            w = jnp.tanh(wx @ p['td_w1']) @ p['td_w2']
            w = jnp.exp(-jnp.exp(p['time_decay'][None, :, None, :] + w.reshape(b, t, H, HS).transpose(0, 2, 1, 3)))
            r4 = r.reshape(b, t, H, HS).transpose(0, 2, 1, 3)
            k4 = k.reshape(b, t, H, HS).transpose(0, 2, 1, 3)
            v4 = v.reshape(b, t, H, HS).transpose(0, 2, 1, 3)
            out = _wkv(r4, k4, v4, w, p['time_first']).transpose(0, 2, 1, 3).reshape(b * t, H, HS)
            mu = out.mean(-1, keepdims=True)
            var = ((out - mu) ** 2).mean(-1, keepdims=True)
            out = ((out - mu) / jnp.sqrt(var + EPS)).reshape(b * t, d) * p['gn_w'] + p['gn_b']
            return out.reshape(b, t, d) * g @ p['Wo']

        def _channel_mix(x, p):
            sx = _shift(x) - x
            k = jnp.square(jax.nn.relu((x + sx * p['ck_maa']) @ p['cWk']))
            return jax.nn.sigmoid((x + sx * p['cr_maa']) @ p['cWr']) * (k @ p['cWv'])
        PER_LAYER = ['ln1_w', 'ln2_w', 'x_maa', 'w_maa', 'k_maa', 'v_maa', 'r_maa', 'g_maa', 'tm_w1', 'tm_w2', 'td_w1', 'td_w2', 'time_decay', 'time_first', 'Wr', 'Wk', 'Wv', 'Wo', 'Wg', 'gn_w', 'gn_b', 'ck_maa', 'cr_maa', 'cWk', 'cWv', 'cWr']

        def _forward(x, params):
            for i in range(L):
                p = {n: params[n][i] for n in PER_LAYER}
                x = x + _time_mix(_ln(x, p['ln1_w']), p)
                x = x + _channel_mix(_ln(x, p['ln2_w']), p)
            return _ln(x, params['ln_out_w'])
        params = dict(ln1_w=ln1_w, ln2_w=ln2_w, x_maa=x_maa, w_maa=w_maa, k_maa=k_maa, v_maa=v_maa, r_maa=r_maa, g_maa=g_maa, tm_w1=tm_w1, tm_w2=tm_w2, td_w1=td_w1, td_w2=td_w2, time_decay=time_decay, time_first=time_first, Wr=Wr, Wk=Wk, Wv=Wv, Wo=Wo, Wg=Wg, gn_w=gn_w, gn_b=gn_b, ck_maa=ck_maa, cr_maa=cr_maa, cWk=cWk, cWv=cWv, cWr=cWr, ln_out_w=ln_out_w)
        return _forward(x, params)

    def _L1_ffn_ref(x, Wqkv, q_scale, k_scale, Wo, ln_g, ln_b, W1, b1, W2, b2):
        import jax, jax.numpy as jnp
        import numpy as np
        DIM = 128
        DEPTH = 6
        HEADS = 16
        DIM_HEAD = 64
        WINDOW = 32
        INNER = HEADS * DIM_HEAD
        DIM_INNER = int(DIM * 4 * 2 / 3)
        QK_SCALE = 8.0

        def shift_tokens(t):
            a, s = jnp.split(t, 2, -1)
            s = jnp.pad(s, ((0, 0), (1, 0), (0, 0)))[:, :-1]
            return jnp.concatenate([a, s], -1)

        def l2norm(t):
            return t / jnp.maximum(jnp.linalg.norm(t, axis=-1, keepdims=True), 1e-12)

        def rotate_half(x):
            x1, x2 = jnp.split(x, 2, -1)
            return jnp.concatenate([-x2, x1], -1)

        def rotary_tables(n):
            half = jnp.arange(0, DIM_HEAD, 2, dtype=jnp.float32)
            inv_freq = 1.0 / 10000.0 ** (half / DIM_HEAD)
            t = jnp.arange(n, dtype=jnp.float32)
            freqs = t[:, None] * inv_freq[None, :]
            freqs = jnp.concatenate([freqs, freqs], -1)
            base_scale = (half + 0.4 * DIM_HEAD) / (1.4 * DIM_HEAD)
            power = (t - n // 2) / (WINDOW // 2)
            scale = base_scale[None, :] ** power[:, None]
            scale = jnp.concatenate([scale, scale], -1)
            return (freqs, scale)

        def local_attention(q, k, v):
            b, h, n, d = q.shape
            w = WINDOW
            nw = n // w
            bq = q.reshape(b, h, nw, w, d)
            bk = k.reshape(b, h, nw, w, d)
            bv = v.reshape(b, h, nw, w, d)

            def look(t):
                p = jnp.pad(t, ((0, 0), (0, 0), (1, 0), (0, 0), (0, 0)))
                return jnp.concatenate([p[:, :, :nw], p[:, :, 1:]], axis=3)
            bk2, bv2 = (look(bk), look(bv))
            seq = jnp.arange(n).reshape(nw, w)
            seq_p = jnp.pad(seq, ((1, 0), (0, 0)), constant_values=-1)
            jt = jnp.concatenate([seq_p[:nw], seq_p[1:]], axis=1)
            it = seq[:, :, None]
            jb = jt[:, None, :]
            mask = (it < jb) | (it > jb + w) | (jb == -1)
            sim = jnp.einsum('bhwie,bhwje->bhwij', bq, bk2) * QK_SCALE
            sim = jnp.where(mask, -jnp.finfo(sim.dtype).max, sim)
            attn = jax.nn.softmax(sim, -1)
            out = jnp.einsum('bhwij,bhwje->bhwie', attn, bv2)
            return out.reshape(b, h, n, d)

        def attn_layer(x, Wqkv, qs, ksc, Wo):
            b, n, _ = x.shape
            qkv = x @ Wqkv
            q, k, v = jnp.split(qkv, 3, -1)
            sh = lambda t: t.reshape(b, n, HEADS, DIM_HEAD).transpose(0, 2, 1, 3)
            q, k, v = (sh(q), sh(k), sh(v))
            q = l2norm(q) * qs
            k = l2norm(k) * ksc
            freqs, scale = rotary_tables(n)
            cos, sin = (jnp.cos(freqs), jnp.sin(freqs))
            q = q * cos * scale + rotate_half(q) * sin * scale
            inv = 1.0 / scale
            k = k * cos * inv + rotate_half(k) * sin * inv
            out = local_attention(q, k, v)
            out = out.transpose(0, 2, 1, 3).reshape(b, n, INNER)
            return out @ Wo

        def ffn_layer(x, g, bln, W1, b1, W2, b2):
            mu = x.mean(-1, keepdims=True)
            var = ((x - mu) ** 2).mean(-1, keepdims=True)
            xn = (x - mu) / jnp.sqrt(var + 1e-05) * g + bln
            hg = xn @ W1 + b1
            a, gate = jnp.split(hg, 2, -1)
            return a * jax.nn.gelu(gate, approximate=False) @ W2 + b2
        for i in range(DEPTH):
            x = attn_layer(shift_tokens(x), Wqkv[i], q_scale[i], k_scale[i], Wo[i]) + x
            x = ffn_layer(shift_tokens(x), ln_g[i], ln_b[i], W1[i], b1[i], W2[i], b2[i]) + x
        return x

    def _L2_attn_ref(x, Wq, bq, Wk, bk, Wv, bv, Wo, bo):
        import jax, jax.numpy as jnp
        import numpy as np
        import math
        NHEAD = 16
        FACTOR = 5
        B, L, Dm = x.shape
        H = NHEAD
        D = Dm // H
        U = min(L, int(FACTOR * math.log(L)) if L > 1 else L)

        def proj(W, b):
            return (x @ W.T + b).reshape(B, L, H, D).transpose(0, 2, 1, 3)
        Q = proj(Wq, bq)
        K = proj(Wk, bk)
        V = proj(Wv, bv)
        scores = jnp.einsum('bhqd,bhkd->bhqk', Q, K) / math.sqrt(D)
        thresh = jax.lax.top_k(scores, U)[0][..., -1:]
        scores = jnp.where(scores < thresh, -jnp.inf, scores)
        attn = jax.nn.softmax(scores, axis=-1)
        context = jnp.einsum('bhqk,bhkd->bhqd', attn, V)
        context = context.transpose(0, 2, 1, 3).reshape(B, L, Dm)
        return context @ Wo.T + bo

    def _L2_ffn_ref(hidden_states, gate_weight, e_bias, gate_proj, up_proj, down_proj):
        import jax, jax.numpy as jnp
        import numpy as np
        TOP_K = 4
        N_GROUP = 4
        TOPK_GROUP = 2
        ROUTED_SCALING = 1.0

        def _route(x_flat, gate_weight, e_bias):
            T = x_flat.shape[0]
            E = gate_weight.shape[0]
            logits = jnp.einsum('th,eh->te', x_flat, gate_weight)
            scores = jax.nn.sigmoid(logits)
            scores_for_choice = scores + e_bias[None, :]
            grp = scores_for_choice.reshape(T, N_GROUP, E // N_GROUP)
            top2, _ = jax.lax.top_k(grp, 2)
            group_scores = top2.sum(axis=-1)
            _, group_idx = jax.lax.top_k(group_scores, TOPK_GROUP)
            group_mask = jax.nn.one_hot(group_idx, N_GROUP, dtype=scores.dtype).sum(axis=1)
            score_mask = jnp.repeat(group_mask, E // N_GROUP, axis=1)
            tmp_scores = jnp.where(score_mask > 0, scores_for_choice, 0.0)
            _, topk_idx = jax.lax.top_k(tmp_scores, TOP_K)
            topk_weight = jnp.take_along_axis(scores, topk_idx, axis=1)
            denom = topk_weight.sum(axis=-1, keepdims=True) + 1e-20
            topk_weight = topk_weight / denom * ROUTED_SCALING
            return (topk_idx, topk_weight)
        B, S, H = hidden_states.shape
        E = gate_proj.shape[0]
        x = hidden_states.reshape(-1, H).astype(jnp.float32)
        topk_idx, topk_weight = _route(x, gate_weight, e_bias)
        combine = (jax.nn.one_hot(topk_idx, E, dtype=x.dtype) * topk_weight[..., None]).sum(axis=1)
        g = jnp.einsum('th,eih->tei', x, gate_proj)
        u = jnp.einsum('th,eih->tei', x, up_proj)
        act = jax.nn.silu(g) * u
        expert_out = jnp.einsum('tei,ehi->teh', act, down_proj)
        y = jnp.einsum('teh,te->th', expert_out, combine)
        return y.reshape(B, S, H)

    def _L3_attn_ref(x, Wkqv, Wm1, bm1, Wm2, bm2, gn_g, gn_b, Wf1, bf1, Wf2, bf2, ln_g, ln_b):
        import jax, jax.numpy as jnp
        import numpy as np
        B, S, D, L = (4, 256, 128, 4)

        def _retention(x, wkqv):
            d = x.shape[-1]
            k, q, v = jnp.split(x @ wkqv, 3, axis=-1)
            qkt = jnp.einsum('bid,bjd->bij', q, k) / jnp.sqrt(jnp.float32(d))
            s = x.shape[1]
            row_norm = 1.0 + jnp.sqrt(jnp.arange(s, dtype=x.dtype))[None, :, None]
            r = jnp.tril(qkt) / row_norm
            denom = jnp.clip(jnp.abs(r.sum(-1, keepdims=True)), 1.0, None)
            r = r / denom
            return jnp.einsum('bij,bjd->bid', r, v)

        def _groupnorm1(y, g, b, eps=1e-05):
            mu = y.mean(axis=(1, 2), keepdims=True)
            var = y.var(axis=(1, 2), keepdims=True)
            return (y - mu) / jnp.sqrt(var + eps) * g + b

        def _layernorm(y, g, b, eps=1e-05):
            mu = y.mean(-1, keepdims=True)
            var = y.var(-1, keepdims=True)
            return (y - mu) / jnp.sqrt(var + eps) * g + b

        def block(h, p):
            wk, w1, b1, w2, b2, gg, gb, wf1, bf1_, wf2, bf2_, lg, lb = p
            r = _retention(h, wk)
            m = r @ w1 + b1
            a, gate = jnp.split(m, 2, axis=-1)
            m = a * jax.nn.silu(gate) @ w2 + b2
            m = _groupnorm1(m, gg, gb)
            y = m + h
            f = jax.nn.gelu(y @ wf1 + bf1_, approximate=False) @ wf2 + bf2_
            return (_layernorm(f + y, lg, lb), None)
        params = (Wkqv, Wm1, bm1, Wm2, bm2, gn_g, gn_b, Wf1, bf1, Wf2, bf2, ln_g, ln_b)
        out, _ = jax.lax.scan(block, x, params)
        return out

    def _L3_ffn_ref(x, router_prob, norm_w, norm_b, q_w, q_b, k_w, k_b, v_w, v_b, o_w, o_b):
        import jax, jax.numpy as jnp
        import numpy as np
        B, T, D, E, H = (4, 256, 128, 4, 8)
        EPS = 1e-05

        def _uniform(k, shape, bound):
            return jax.random.uniform(k, shape, jnp.float32, -bound, bound)

        def _layernorm(x, w, b):
            mu = jnp.mean(x, axis=-1, keepdims=True)
            var = jnp.mean(jnp.square(x - mu), axis=-1, keepdims=True)
            return (x - mu) * jax.lax.rsqrt(var + EPS) * w + b
        e_cnt = router_prob.shape[2]
        b, t, d = x.shape
        n = t // e_cnt
        h = H
        scale = d ** (-0.5)
        qs, ks_, vs = ([], [], [])
        for e in range(e_cnt):
            xe = x[:, e * n:(e + 1) * n, :]
            xn = _layernorm(xe, norm_w, norm_b)
            m = d // 2 ** e
            xm = xn[..., :m]
            qs.append(jnp.einsum('bnm,dm->bnd', xm, q_w[:, :m]) + q_b)
            ks_.append(jnp.einsum('bnm,dm->bnd', xm, k_w[:, :m]) + k_b)
            vs.append(jnp.einsum('bnm,dm->bnd', xm, v_w[:, :m]) + v_b)
        q = jnp.concatenate(qs, axis=1)
        k = jnp.concatenate(ks_, axis=1)
        v = jnp.concatenate(vs, axis=1)
        dh = d // h
        q = q.reshape(b, t, h, dh).transpose(0, 2, 1, 3)
        k = k.reshape(b, t, h, dh).transpose(0, 2, 1, 3)
        v = v.reshape(b, t, h, dh).transpose(0, 2, 1, 3)
        attn = jnp.einsum('bhqd,bhkd->bhqk', q, k) * scale
        attn = jax.nn.softmax(attn, axis=-1)
        attn_out = jnp.einsum('bhqk,bhkd->bhqd', attn, v)
        attn_out = attn_out.transpose(0, 2, 1, 3).reshape(b, t, d)
        outs = []
        for e in range(e_cnt):
            sl = slice(e * n, (e + 1) * n)
            m = d // 2 ** e
            xm = attn_out[:, sl, :m]
            out = jnp.einsum('bnm,om->bno', xm, o_w[:m, :m]) + o_b[:m]
            pad = d - m
            if pad:
                out = jnp.pad(out, ((0, 0), (0, 0), (0, pad)))
            outs.append(out + x[:, sl, :])
        return jnp.concatenate(outs, axis=1)
    x = L0_attn_x
    xn = _layernorm(x, axis=-1)
    s = _L0_attn_ref(xn, L0_attn_W_in, L0_attn_conv_w, L0_attn_conv_b, L0_attn_W_gates, L0_attn_b_gates, L0_attn_forget_base, L0_attn_W_out)
    g = _silu(_L0_ffn_ref(xn, L0_ffn_weight, L0_ffn_disha))
    x = x + s * g
    xn = _layernorm(x, axis=-1)
    s = _L1_attn_ref(xn, L1_attn_ln1_w, L1_attn_ln2_w, L1_attn_x_maa, L1_attn_w_maa, L1_attn_k_maa, L1_attn_v_maa, L1_attn_r_maa, L1_attn_g_maa, L1_attn_tm_w1, L1_attn_tm_w2, L1_attn_td_w1, L1_attn_td_w2, L1_attn_time_decay, L1_attn_time_first, L1_attn_Wr, L1_attn_Wk, L1_attn_Wv, L1_attn_Wo, L1_attn_Wg, L1_attn_gn_w, L1_attn_gn_b, L1_attn_ck_maa, L1_attn_cr_maa, L1_attn_cWk, L1_attn_cWv, L1_attn_cWr, L1_attn_ln_out_w)
    g = _silu(_L1_ffn_ref(xn, L1_ffn_Wqkv, L1_ffn_q_scale, L1_ffn_k_scale, L1_ffn_Wo, L1_ffn_ln_g, L1_ffn_ln_b, L1_ffn_W1, L1_ffn_b1, L1_ffn_W2, L1_ffn_b2))
    x = x + s * g
    xn = _layernorm(x, axis=-1)
    s = _L2_attn_ref(xn, L2_attn_Wq, L2_attn_bq, L2_attn_Wk, L2_attn_bk, L2_attn_Wv, L2_attn_bv, L2_attn_Wo, L2_attn_bo)
    g = _silu(_L2_ffn_ref(xn, L2_ffn_gate_weight, L2_ffn_e_bias, L2_ffn_gate_proj, L2_ffn_up_proj, L2_ffn_down_proj))
    x = x + s * g
    xn = _layernorm(x, axis=-1)
    s = _L3_attn_ref(xn, L3_attn_Wkqv, L3_attn_Wm1, L3_attn_bm1, L3_attn_Wm2, L3_attn_bm2, L3_attn_gn_g, L3_attn_gn_b, L3_attn_Wf1, L3_attn_bf1, L3_attn_Wf2, L3_attn_bf2, L3_attn_ln_g, L3_attn_ln_b)
    g = _silu(_L3_ffn_ref(xn, L3_ffn_router_prob, L3_ffn_norm_w, L3_ffn_norm_b, L3_ffn_q_w, L3_ffn_q_b, L3_ffn_k_w, L3_ffn_k_b, L3_ffn_v_w, L3_ffn_v_b, L3_ffn_o_w, L3_ffn_o_b))
    x = x + s * g
    return x

_drawn_inputs = setup_inputs


def setup_inputs(seed=0):
    import zlib

    import numpy as np

    out = dict(_drawn_inputs(seed))
    spreads = {'L0_attn_b_gates': (0.0, 0.514),
     'L1_attn_ln1_w': (1.0, 0.6),
     'L1_attn_ln2_w': (1.0, 0.6),
     'L1_attn_gn_w': (1.0, 0.6),
     'L1_attn_gn_b': (0.0, 0.8),
     'L1_attn_ln_out_w': (1.0, 0.2),
     'L1_ffn_q_scale': (1.0, 0.6),
     'L1_ffn_k_scale': (1.0, 0.6),
     'L1_ffn_ln_g': (1.0, 0.6),
     'L1_ffn_ln_b': (0.0, 0.8),
     'L1_ffn_b1': (0.0, 0.8),
     'L1_ffn_b2': (0.0, 0.1),
     'L2_ffn_e_bias': (0.0, 0.8),
     'L3_attn_bm1': (0.0, 0.8),
     'L3_attn_bm2': (0.0, 0.1),
     'L3_attn_gn_g': (1.0, 0.2),
     'L3_attn_gn_b': (0.0, 0.1),
     'L3_attn_bf1': (0.0, 0.8),
     'L3_attn_bf2': (0.0, 0.267),
     'L3_attn_ln_g': (1.0, 0.2),
     'L3_attn_ln_b': (0.0, 0.1),
     'L3_ffn_norm_w': (1.0, 0.6),
     'L3_ffn_norm_b': (0.0, 0.8)}
    factors = {'L1_attn_x_maa': 8.0,
     'L1_attn_w_maa': 8.0,
     'L1_attn_k_maa': 8.0,
     'L1_attn_v_maa': 8.0,
     'L1_attn_r_maa': 8.0,
     'L1_attn_g_maa': 8.0,
     'L1_attn_tm_w1': 8.0,
     'L1_attn_tm_w2': 8.0,
     'L1_attn_td_w1': 8.0,
     'L1_attn_td_w2': 8.0,
     'L1_attn_time_decay': 6.288,
     'L1_attn_time_first': 8.0,
     'L1_attn_Wr': 8.0,
     'L1_attn_Wk': 4.852,
     'L1_attn_Wv': 4.657,
     'L1_attn_Wo': 4.509,
     'L1_attn_Wg': 4.639,
     'L1_attn_ck_maa': 8.0,
     'L1_attn_cr_maa': 8.0,
     'L1_attn_cWk': 8.0,
     'L1_attn_cWv': 8.0,
     'L1_attn_cWr': 8.0,
     'L1_ffn_W1': 3.985,
     'L1_ffn_W2': 3.923,
     'L2_attn_Wq': 8.0,
     'L2_attn_bq': 8.0,
     'L2_attn_Wk': 8.0,
     'L2_attn_bk': 64.0,
     'L2_attn_Wv': 8.0,
     'L2_attn_bv': 8.0,
     'L2_attn_Wo': 8.0,
     'L2_attn_bo': 8.0,
     'L2_ffn_gate_weight': 8.0,
     'L2_ffn_gate_proj': 8.0,
     'L2_ffn_up_proj': 8.0,
     'L2_ffn_down_proj': 8.0,
     'L3_attn_Wkqv': 8.0,
     'L3_attn_Wm1': 8.0,
     'L3_attn_Wm2': 8.0,
     'L3_attn_Wf1': 3.472,
     'L3_attn_Wf2': 3.246,
     'L3_ffn_q_w': 8.0,
     'L3_ffn_q_b': 8.0,
     'L3_ffn_k_w': 8.0,
     'L3_ffn_k_b': 64.0,
     'L3_ffn_v_w': 8.0,
     'L3_ffn_v_b': 8.0,
     'L3_ffn_o_w': 8.0,
     'L3_ffn_o_b': 28.628}
    for name, (base, spread) in spreads.items():
        noise = np.random.default_rng([zlib.crc32(name.encode()), seed]).standard_normal(out[name].shape)
        drawn = base * np.exp(spread * noise) if base else spread * noise
        out[name] = jnp.asarray(drawn.astype(out[name].dtype))
    for name, factor in factors.items():
        out[name] = (out[name] * factor).astype(out[name].dtype)
    return out
```

```python
from contextlib import ExitStack, contextmanager

import numpy as np
import concourse.bass as bass
from concourse import mybir

F32 = mybir.dt.float32
ALU = mybir.AluOpType
ACT = mybir.ActivationFunctionType
AX = mybir.AxisListType

P = 128
BATCH = 4
SEQ = 512
TOK = BATCH * SEQ
NSLAB = 20
LN_EPS = 1e-5


def offsets(parts):
    at, where = 0, {}
    for name, width in parts:
        where[name] = (at, width)
        at += width
    return where, at


CONST_PARTS = [("mean", P), ("ident", P), ("halves", P), ("mean_halves", P), ("tiny", 4), ("ones_row", P)]

HID = 192
HC = 96
L0_PARTS = [("w_gate", HID), ("w_x", HID), ("w_gates0", 2 * HID), ("w_gates1", 2 * HID),
            ("w_out0", P), ("w_out1", P), ("ffn", P), ("disha", P),
            ("conv_w", 8), ("conv_b", 2), ("b_forget", 2), ("b_inp", 2), ("forget_base", 2)]


RAISED = 1


@contextmanager
def phase(nc, names, raised=False):
    with ExitStack() as ctx:
        sems = [ctx.enter_context(nc.semaphore(n)) for n in names.split()]
        if raised:
            for s in sems:
                nc.sync.sem_inc(s, RAISED)
            nc.all_engine_barrier()
        with nc.Block(no_gpsimd_drain=True) as block:
            yield (block, *sems)
        for s in sems:
            nc.sync.sem_clear(s)
        nc.all_engine_barrier()


class Chain:

    def __init__(self, engine, sem, base=0, passed=None):
        self.engine, self.sem, self.base, self.n, self.passed = engine, sem, base, 0, passed

    def __call__(self, ins):
        ins.then_inc(self.sem, 1)
        self.n += 1
        self.engine.wait_ge(self.sem, self.base + self.n)
        if self.passed is not None:
            hold(self.engine, self.passed)


def hold(engine, passed):
    engine.sem_inc(passed, 1)


def cols(b):
    return slice(b * SEQ, (b + 1) * SEQ)


def layer_norm(nc, m, src, dst, gamma=None, beta=None, tag="ln", mean=None, refine=True):
    ps, cen, sq, step = m.psum, m.slab(NSLAB - 1), m.slab(NSLAB - 2), m.slab(NSLAB - 3)
    mean = m.mean if mean is None else mean
    with phase(nc, f"{tag}_mean {tag}_centred {tag}_squared {tag}_var {tag}_std {tag}_own {tag}_normed") as (
            block, mean_ready, centred, squared, var_ready, std_ready, own, normed):
        @block.tensor
        def _(pe):
            for b in range(BATCH):
                nc.tensor.matmul(ps[:, b, :], mean, src[:, cols(b)], start=True, stop=True).then_inc(mean_ready, 1)
            for b in range(BATCH):
                pe.wait_ge(squared, b + 1)
                nc.tensor.matmul(ps[:, 4 + b, :], mean, sq[:, cols(b)], start=True, stop=True).then_inc(var_ready, 1)

        @block.scalar
        def _(act):
            for b in range(BATCH):
                act.wait_ge(centred, b + 1)
                nc.scalar.activation(sq[:, cols(b)], cen[:, cols(b)], ACT.Square).then_inc(squared, 1)
            for b in range(BATCH):
                act.wait_ge(var_ready, b + 1)
                nc.scalar.activation(sq[:, cols(b)], ps[:, 4 + b, :], ACT.Sqrt, bias=m.tiny[:, 0:1]).then_inc(std_ready, 1)
            if beta is not None:
                for b in range(BATCH):
                    act.wait_ge(normed, b + 1)
                    nc.scalar.activation(dst[:, cols(b)], cen[:, cols(b)], ACT.Identity, bias=beta)

        @block.vector
        def _(dve):
            link = Chain(dve, own)
            for b in range(BATCH):
                dve.wait_ge(mean_ready, b + 1)
                nc.vector.tensor_tensor(cen[:, cols(b)], src[:, cols(b)], ps[:, b, :], ALU.subtract).then_inc(centred, 1)
            for b in range(BATCH):
                dve.wait_ge(std_ready, b + 1)
                r, t = sq[:, cols(b)], step[:, cols(b)]
                link(nc.vector.reciprocal(r, r))
                if refine:
                    link(nc.vector.tensor_tensor(t, r, r, ALU.mult))
                    link(nc.vector.scalar_tensor_tensor(out=t, in0=ps[:, 4 + b, :], scalar=LN_EPS, in1=t, op0=ALU.add, op1=ALU.mult))
                    link(nc.vector.tensor_scalar(t, t, -0.5, 1.5, ALU.mult, ALU.add))
                    link(nc.vector.tensor_tensor(r, r, t, ALU.mult))
                out = dst if beta is None else cen
                if b == 0:
                    dve.wait_ge(centred, BATCH)
                if gamma is None:
                    nc.vector.tensor_tensor(out[:, cols(b)], cen[:, cols(b)], sq[:, cols(b)], ALU.mult).then_inc(normed, 1)
                else:
                    nc.vector.scalar_tensor_tensor(out=out[:, cols(b)], in0=cen[:, cols(b)], scalar=gamma,
                                                   in1=sq[:, cols(b)], op0=ALU.mult, op1=ALU.mult).then_inc(normed, 1)


def add_product(nc, x, s, g, tag="residual"):
    with phase(nc, f"{tag}_gated") as (block, gated):
        @block.gpsimd
        def _(pool):
            for b in range(BATCH):
                nc.gpsimd.tensor_tensor(s[:, cols(b)], s[:, cols(b)], g[:, cols(b)], ALU.mult).then_inc(gated, 1)

        @block.vector
        def _(dve):
            for b in range(BATCH):
                dve.wait_ge(gated, b + 1)
                nc.vector.tensor_tensor(x[:, cols(b)], x[:, cols(b)], s[:, cols(b)], ALU.add)


class Memory:

    def __init__(self, nc, ctx):
        self.nc = nc
        self.slabs = ctx.enter_context(nc.sbuf_tensor("slabs", [P, NSLAB * TOK], F32))
        where, width = offsets(CONST_PARTS)
        self.const = ctx.enter_context(nc.sbuf_tensor("constants", [P, width], F32))
        self.psum = ctx.enter_context(nc.psum_tensor("psum", [P, 8, 512], F32))
        self.masks = ctx.enter_context(nc.sbuf_tensor("window_masks", [P, 320], F32))[:, :]
        self.weights = ctx.enter_context(nc.sbuf_tensor("weights", [P, 5632], F32))

        def constant(name, rows=P):
            at, n = where[name]
            return self.const[0:rows, at:at + n]

        self.mean, self.ident = constant("mean"), constant("ident")
        self.halves, self.mean_halves = constant("halves"), constant("mean_halves")
        self.tiny, self.ones_row = constant("tiny"), constant("ones_row", 1)

    def slab(self, i, n=1):
        return self.slabs[:, i * TOK:(i + n) * TOK]


def load(nc, pairs, tag):
    with phase(nc, f"{tag}_loaded") as (block, loaded):
        @block.sync
        def _(sp):
            for dst, src in pairs:
                sp.dma_start(dst, src).then_inc(loaded, 16)
            sp.wait_ge(loaded, 16 * len(pairs))


def block0(nc, m, ins, x):
    where, width = offsets(L0_PARTS)
    W = m.weights
    load(nc, [(W[:, 0:width], ins["L0"])], "l0")

    def w(name, a=0, n=None, rows=P):
        o, width = where[name]
        return W[0:rows, o + a:o + (a + n if n else width)]

    xn = m.slab(1)
    layer_norm(nc, m, x, xn, tag="l0ln")

    ps = m.psum
    gate = m.slab(2, 2).rearrange("p (c t) -> p c t", c=2)
    conv = m.slab(4, 2).rearrange("p (c t) -> p c t", c=2)
    ffn = m.slab(6)
    PADDED = SEQ + 3
    xh = m.slab(7, 3)[:, 0:2 * BATCH * PADDED].rearrange("p (u t) -> p u t", t=PADDED)
    forget = m.slab(10, 2).rearrange("p (c t) -> p c t", c=2)
    inp = m.slab(12, 2).rearrange("p (c t) -> p c t", c=2)
    beta = m.slab(14, 2).rearrange("p (c t) -> p c t", c=2)
    units = [(c, b) for c in range(2) for b in range(BATCH)]

    with phase(nc, "x_product x_copied gate_product gate_done ffn_product conv_step padded tanh_done") as (
            block, x_product, x_copied, gate_product, gate_done, ffn_product, conv_step, padded, tanh_done):
        @block.tensor
        def _(pe):
            for n, (c, b) in enumerate(units):
                nc.tensor.matmul(ps[0:HC, n, :], w("w_x", c * HC, HC), xn[:, cols(b)],
                                 start=True, stop=True).then_inc(x_product, 1)
            for n, (c, b) in enumerate(units):
                pe.wait_ge(x_copied, n + 1)
                nc.tensor.matmul(ps[0:HC, n, :], w("w_gate", c * HC, HC), xn[:, cols(b)],
                                 start=True, stop=True).then_inc(gate_product, 1)
            for b in range(BATCH):
                pe.wait_ge(gate_done, b + 1)
                nc.tensor.matmul(ps[:, b, :], w("ffn"), xn[:, cols(b)], start=True, stop=False)
                nc.tensor.matmul(ps[:, b, :], w("disha"), xn[:, cols(b)],
                                 start=False, stop=True).then_inc(ffn_product, 1)

        @block.vector
        def _(dve):
            link = Chain(dve, conv_step)
            nc.vector.memset(xh[0:HC, :, 0:3], 0.0).then_inc(padded, 1)
            for n in range(8):
                dve.wait_ge(x_product, n + 1)
                nc.vector.tensor_copy(xh[0:HC, n, 3:PADDED], ps[0:HC, n, :]).then_inc(x_copied, 1)
            dve.wait_ge(padded, 1)
            for n, (c, b) in enumerate(units):
                dve.wait_ge(x_copied, n + 1)
                y = conv[0:HC, c, cols(b)]
                link(nc.vector.tensor_scalar(y, xh[0:HC, n, 0:SEQ], w("conv_w", 4 * c, 1, HC),
                                             w("conv_b", c, 1, HC), ALU.mult, ALU.add))
                for k in range(1, 4):
                    link(nc.vector.scalar_tensor_tensor(out=y, in0=xh[0:HC, n, k:k + SEQ],
                                                        scalar=w("conv_w", 4 * c + k, 1, HC), in1=y,
                                                        op0=ALU.mult, op1=ALU.add))
            for b in range(BATCH):
                dve.wait_ge(tanh_done, b + 1)
                nc.vector.scalar_tensor_tensor(out=ffn[:, cols(b)], in0=ffn[:, cols(b)], scalar=1.0, in1=ps[:, b, :],
                                               op0=ALU.add, op1=ALU.mult)

        @block.scalar
        def _(act):
            for n, (c, b) in enumerate(units):
                act.wait_ge(gate_product, n + 1)
                nc.scalar.activation(gate[0:HC, c, cols(b)], ps[0:HC, n, :], ACT.Gelu).then_inc(gate_done, 1)
            for b in range(BATCH):
                act.wait_ge(ffn_product, b + 1)
                nc.scalar.activation(ffn[:, cols(b)], ps[:, b, :], ACT.Tanh, scale=0.5).then_inc(tanh_done, 1)

    rate = m.slab(16)[:, 0:2]
    tmp = m.slab(16)[:, 4:12]
    halved = m.slab(16)[:, 12:16]
    with phase(nc, "gates_product gates_done rate_exp rate_ready rate_step alpha_ready alpha_sq beta_ready state_step") as (
            block, gates_product, gates_done, rate_exp, rate_ready, rate_step, alpha_ready, alpha_sq, beta_ready, state_step):
        @block.tensor
        def _(pe):
            for k in range(2):
                for n, (c, b) in enumerate(units):
                    if k:
                        pe.wait_ge(gates_done, n + 1)
                    col = k * HID + c * HC
                    nc.tensor.matmul(ps[0:HC, n, :], w("w_gates0", col, HC, HC), conv[0:HC, 0, cols(b)], start=True, stop=False)
                    nc.tensor.matmul(ps[0:HC, n, :], w("w_gates1", col, HC, HC), conv[0:HC, 1, cols(b)],
                                     start=False, stop=True).then_inc(gates_product, 1)

        @block.scalar
        def _(act):
            link = Chain(act, rate_exp)
            link(nc.scalar.activation(tmp[0:HC, 0:2], w("forget_base", 0, 2, HC), ACT.Abs))
            link(nc.scalar.activation(tmp[0:HC, 0:2], tmp[0:HC, 0:2], ACT.Tanh, scale=-1.0 / 32))
            for k in range(2):
                dst, bias = (forget, "b_forget") if k == 0 else (inp, "b_inp")
                for n, (c, b) in enumerate(units):
                    act.wait_ge(gates_product, 8 * k + n + 1)
                    if k == 0 and n == 0:
                        act.wait_ge(rate_ready, 1)
                    nc.scalar.activation(dst[0:HC, c, cols(b)], ps[0:HC, n, :], ACT.Tanh, scale=0.5,
                                         bias=halved[0:HC, 2 * k + c:2 * k + c + 1]).then_inc(gates_done, 1)
            for n, (c, b) in enumerate(units):
                act.wait_ge(gates_done, n + 1)
                nc.scalar.activation(forget[0:HC, c, cols(b)], forget[0:HC, c, cols(b)], ACT.Tanh,
                                     scale=rate[0:HC, c:c + 1], bias=rate[0:HC, c:c + 1]).then_inc(alpha_ready, 1)
            for n, (c, b) in enumerate(units):
                act.wait_ge(alpha_sq, n + 1)
                nc.scalar.activation(beta[0:HC, c, cols(b)], beta[0:HC, c, cols(b)], ACT.Sqrt,
                                     bias=m.tiny[0:HC, 1:2]).then_inc(beta_ready, 1)

        @block.vector
        def _(dve):
            dve.wait_ge(rate_exp, 2)
            link = Chain(dve, rate_step)
            t, e, s2 = tmp[0:HC, 0:2], tmp[0:HC, 2:4], tmp[0:HC, 4:6]
            link(nc.vector.tensor_scalar(e, t, -1.0, 1.0, ALU.mult, ALU.add))
            link(nc.vector.reciprocal(e, e))
            link(nc.vector.scalar_tensor_tensor(out=e, in0=t, scalar=1.0, in1=e, op0=ALU.add, op1=ALU.mult))
            for _ in range(4):
                link(nc.vector.tensor_tensor(e, e, e, ALU.mult))
            link(nc.vector.tensor_scalar(t, e, 2.0, None, ALU.add))
            link(nc.vector.reciprocal(t, t))
            link(nc.vector.tensor_tensor(e, e, t, ALU.mult))
            link(nc.vector.tensor_tensor(s2, e, e, ALU.mult))
            link(nc.vector.tensor_scalar(t, s2, 1.0 / 15, None, ALU.mult))
            for k in (13, 11, 9, 7, 5, 3):
                link(nc.vector.scalar_tensor_tensor(out=t, in0=t, scalar=1.0 / k, in1=s2, op0=ALU.add, op1=ALU.mult))
            link(nc.vector.scalar_tensor_tensor(out=t, in0=t, scalar=1.0, in1=e, op0=ALU.add, op1=ALU.mult))
            link(nc.vector.tensor_scalar(e, w("forget_base", 0, 2, HC), 0.0, None, ALU.max))
            link(nc.vector.scalar_tensor_tensor(out=rate[0:HC, :], in0=t, scalar=2.0, in1=e, op0=ALU.mult, op1=ALU.add))
            link(nc.vector.tensor_scalar(halved[0:HC, 0:2], w("b_forget", 0, 2, HC), 0.5, None, ALU.mult))
            link(nc.vector.tensor_scalar(halved[0:HC, 2:4], w("b_inp", 0, 2, HC), 0.5, None, ALU.mult))
            nc.vector.tensor_scalar(rate[0:HC, :], rate[0:HC, :], -2.0, None, ALU.mult).then_inc(rate_ready, 1)
            for n, (c, b) in enumerate(units):
                dve.wait_ge(alpha_ready, n + 1)
                y, a = beta[0:HC, c, cols(b)], forget[0:HC, c, cols(b)]
                link(nc.vector.tensor_scalar(y, a, -1.0, 1.0, ALU.mult, ALU.add))
                link(nc.vector.reciprocal(y, y))
                link(nc.vector.tensor_tensor(a, a, y, ALU.mult))
                link(nc.vector.tensor_scalar(a, a, 2.0, 1.0, ALU.mult, ALU.add))
                link(nc.vector.tensor_tensor(y, a, a, ALU.mult))
                nc.vector.tensor_scalar(y, y, -1.0, 1.0, ALU.mult, ALU.add).then_inc(alpha_sq, 1)
            link = Chain(dve, state_step)
            dve.wait_ge(gates_done, 16)
            for n, (c, b) in enumerate(units):
                y = beta[0:HC, c, cols(b)]
                dve.wait_ge(beta_ready, n + 1)
                link(nc.vector.scalar_tensor_tensor(out=y, in0=inp[0:HC, c, cols(b)], scalar=1.0, in1=y, op0=ALU.add, op1=ALU.mult))
                link(nc.vector.scalar_tensor_tensor(out=y, in0=y, scalar=0.5, in1=conv[0:HC, c, cols(b)], op0=ALU.mult, op1=ALU.mult))
                link(nc.vector.tensor_tensor_scan(y, forget[0:HC, c, cols(b)], y, 0.0, ALU.mult, ALU.add))
                link(nc.vector.tensor_tensor(gate[0:HC, c, cols(b)], gate[0:HC, c, cols(b)], y, ALU.mult))

    with phase(nc, "out_product out_step") as (block, out_product, out_step):
        @block.tensor
        def _(pe):
            for b in range(BATCH):
                nc.tensor.matmul(ps[:, b, :], w("w_out0", rows=HC), gate[0:HC, 0, cols(b)], start=True, stop=False)
                nc.tensor.matmul(ps[:, b, :], w("w_out1", rows=HC), gate[0:HC, 1, cols(b)],
                                 start=False, stop=True).then_inc(out_product, 1)

        @block.vector
        def _(dve):
            link = Chain(dve, out_step)
            for b in range(BATCH):
                dve.wait_ge(out_product, b + 1)
                link(nc.vector.scalar_tensor_tensor(out=ffn[:, cols(b)], in0=ffn[:, cols(b)], scalar=0.5, in1=ps[:, b, :],
                                                    op0=ALU.mult, op1=ALU.mult))
                link(nc.vector.tensor_tensor(x[:, cols(b)], x[:, cols(b)], ffn[:, cols(b)], ALU.add))


HEADS1, HD1 = 16, 64
PADSEQ = SEQ + 1
FF1 = 341
F1_PARTS = [("qk", 8 * 4 * P), ("v", HEADS1 * HD1), ("out", HEADS1 * HD1), ("up", 6 * P), ("down", 3 * P),
            ("scales", 4), ("ln_g", 1), ("ln_b", 1), ("b_up", 6), ("b_down", 1)]
FF1_ROWS = [P, P, FF1 - 2 * P]
REACH = 32
MASKED = -2.0 ** 120


def local_transformer(nc, m, ins, xn, g_out):
    where, width = offsets(F1_PARTS)
    W = m.slab(2, 4)[:, 0:width]
    tables = m.slab(6).rearrange("p (k t) -> p k t", k=4)
    scaled = m.slab(7).rearrange("p (k t) -> p k t", k=4)
    hA = m.slab(8, 2)[:, 0:BATCH * PADSEQ].rearrange("p (b t) -> p b t", b=BATCH)
    hB = m.slab(10, 2)[:, 0:BATCH * PADSEQ].rearrange("p (b t) -> p b t", b=BATCH)

    def w(name, a=0, n=None, rows=P):
        o, width = where[name]
        return W[0:rows, o + a:o + (a + n if n else width)]

    with phase(nc, "tables_loaded residual_padded") as (block, tables_loaded, residual_padded):
        @block.sync
        def _(sp):
            sp.dma_start(m.slab(6), ins["rotary"]).then_inc(tables_loaded, 16)
            sp.dma_start(m.masks, ins["masks"]).then_inc(tables_loaded, 16)
            sp.wait_ge(tables_loaded, 32)

        @block.vector
        def _(dve):
            nc.vector.memset(hA[:, :, 0:1], 0.0)
            nc.vector.memset(hB[:, :, 0:1], 0.0)
            nc.vector.tensor_copy(hA[:, :, 1:PADSEQ], xn.rearrange("p (b t) -> p b t", b=BATCH))

        @block.gpsimd
        def _(pool):
            nc.gpsimd.memset(m.slab(12, 5), 0.0)

    with nc.Fori(0, 6) as layer:
        with phase(nc, "layer_loaded tables_scaled") as (block, layer_loaded, tables_scaled):
            @block.sync
            def _(sp):
                sp.dma_start(W, ins["F1"][bass.ds(layer, 1)].rearrange("l p n -> (l p) n")).then_inc(layer_loaded, 16)

            @block.scalar
            def _(act):
                act.wait_ge(layer_loaded, 16)
                for k in range(4):
                    nc.scalar.activation(scaled[:, k, :], tables[:, k, :], ACT.Copy, scale=w("scales", k, 1))
        local_attention(nc, m, w, scaled, hA, hB)
        shift_tokens(nc, hB, m.slab(12))
        layer_norm(nc, m, m.slab(12), m.slab(13), w("ln_g"), w("ln_b"), tag="f1")
        gated_feed_forward(nc, m, w, m.slab(13), hB, hA)

    with phase(nc, "silu_done") as (block, silu_done):
        @block.scalar
        def _(act):
            nc.scalar.activation(g_out.rearrange("p (b t) -> p b t", b=BATCH), hA[:, :, 1:PADSEQ], ACT.Silu)


def local_attention(nc, m, w, tables, hA, hB):
    ps = m.psum
    xs = m.slab(12)[:, 0:P]
    mask_even = m.slab(12)[:, P:P + 160]
    v = [m.slab(12 + p)[:, 512:512 + HEADS1 * 65].rearrange("p (h d) -> p h d", h=HEADS1) for p in range(2)]
    qk = [m.slab(14 + p).rearrange("p (c k t) -> p c k t", c=8, k=2) for p in range(2)]
    probs = [m.slab(16)[:, 512 * n:512 * n + 512].rearrange("p (h k) -> p h k", h=2) for n in range(2)]
    probsT = [m.slab(16)[:, 1024 + 512 * n:1536 + 512 * n].rearrange("p (h k q) -> p h k q", h=2, k=2) for n in range(2)]
    squares = m.slab(17)[:, 0:1024].rearrange("p (c k t) -> p c k t", c=4, k=2)
    norms = [a.rearrange("p (c k t) -> p c k t", c=4, k=2) for a in (m.slab(17)[:, 1024:2048], m.weights[:, 0:1024])]
    rotated = [a.rearrange("p (c k t) -> p c k t", c=4, k=2) for a in (m.slab(18)[:, 0:1024], m.weights[:, 1024:2048])]
    context = m.slab(18)[:, 1024:2048]
    contextT = m.slab(19)[:, 0:1024].rearrange("p (c t) -> p c t", c=8)
    scores = [m.slab(19)[:, 1024 + 320 * n:1344 + 320 * n].rearrange("p (h k) -> p h k", h=2) for n in range(2)]
    small = [m.slab(19)[:, 1664 + 8 * n:1672 + 8 * n] for n in range(2)]
    QK = ps[:, 0:4, :].rearrange("p c (k t) -> p c k t", k=4)
    SS = ps[:, 4:6, :].rearrange("p b (c k t) -> p (b c) k t", c=2, k=2)
    V = ps[:, 6:8, :].rearrange("p b (h d) -> p (b h) d", d=HD1)

    def S(n, h):
        return ps[:, 2 + 2 * (n % 2) + h, 0:160]

    def PT(n):
        return ps[:, 6 + n % 2, :].rearrange("p (h k q) -> p h k q", h=2, k=2)

    def CTX(n):
        return ps[:, n % 2, 0:130].rearrange("p (h d) -> p h d", h=2)

    CT = ps[:, 4:6, :].rearrange("p b (c t) -> p (b c) t", c=4)
    OUT = ps[:, 6, 0:P]
    PAIRS = HEADS1 // 2

    def tiles(engine, body):
        with engine.Fori(0, BATCH) as b:
            with engine.Fori(0, 2) as t2:
                for parity in range(2):
                    body(b, t2, parity, b * 4 + t2 * 2 + parity)

    with phase(nc, "ones_ready xs_ready mask_ready qk_product squared norm2_product norm_ready inv_ready rope_product "
                   "qk_ready v_product v_copied score_product masked negmax_ready exp_done "
                   "pT_ready pT_copied pv_done ctx_copied ctxT_ready ctxT_copied out_product resid_done step recip_step dve_passed",
               raised=True) as (
            block, ones_ready, xs_ready, mask_ready, qk_product, squared, norm2_product, norm_ready, inv_ready, rope_product,
            qk_ready, v_product, v_copied, score_product, masked, negmax_ready, exp_done,
            pT_ready, pT_copied, pv_done, ctx_copied, ctxT_ready, ctxT_copied, out_product, resid_done, step, recip_step, dve_passed):

        @block.gpsimd
        def _(pool):
            def tile(b, t2, parity, g):
                if parity == 0:
                    pool.wait_ge(masked, g * PAIRS + RAISED)
                    nc.gpsimd.tensor_copy(mask_even, m.masks[:, bass.ds(t2 * 160, 160)]).then_inc(mask_ready, 1)
                for j in range(2):
                    pool.wait_ge(rope_product, 4 * g + 2 * j + 2 + RAISED)
                    out = qk[parity][:, 4 * j:4 * j + 4, :, :]
                    nc.gpsimd.tensor_tensor(out, out, rotated[j], ALU.add).then_inc(step, 1)
                    pool.wait_ge(step, 2 * g + j + 1 + RAISED)
                    pool.wait_ge(inv_ready, 5 * g + 4 * j + 1 + RAISED)
                    nc.gpsimd.tensor_tensor(out, out, norms[j], ALU.mult).then_inc(qk_ready, 1)
            tiles(pool, tile)

        @block.tensor
        def _(pe):
            def tile(b, t2, parity, g):
                def project(j):
                    if j == 0:
                        pe.wait_ge(ctx_copied, PAIRS * g + RAISED)
                        pe.wait_ge(xs_ready, 2 * g + 2 + RAISED)
                    else:
                        pe.wait_ge(rope_product, 4 * g + 2 + RAISED)
                        pe.wait_ge(squared, 2 * g + 1 + RAISED)
                    for c in range(4):
                        for k in range(4):
                            last = nc.tensor.matmul(QK[:, c, k, :], w("qk", ((4 * j + c) * 4 + k) * P, P), xs,
                                                    start=True, stop=True)
                    last.then_inc(qk_product, 1)

                def norm2(j):
                    pe.wait_ge(squared, 2 * g + j + 1 + RAISED)
                    if j == 0:
                        pe.wait_ge(ctxT_copied, g + RAISED)
                    else:
                        pe.wait_ge(norm_ready, 2 * g + 1 + RAISED)
                    for c in range(2):
                        last = nc.tensor.matmul(ps[:, 4 + c, :], m.halves, squares[:, 2 * c:2 * c + 2, :, :],
                                                start=True, stop=True)
                    last.then_inc(norm2_product, 1)

                def values():
                    pe.wait_ge(resid_done, g + RAISED)
                    for c in range(2):
                        last = nc.tensor.matmul(ps[:, 6 + c, :], xs, w("v", 512 * c, 512), start=True, stop=True)
                    last.then_inc(v_product, 1)

                def score(n):
                    if n == 0:
                        pe.wait_ge(qk_ready, 2 * g + 1 + RAISED)
                        pe.wait_ge(rope_product, 4 * g + 4 + RAISED)
                    if n == 1:
                        pe.wait_ge(norm_ready, 2 * g + 2 + RAISED)
                    if n == PAIRS // 2:
                        pe.wait_ge(qk_ready, 2 * g + 2 + RAISED)
                    if n >= 2:
                        pe.wait_ge(masked, PAIRS * g + n - 1 + RAISED)
                    for h in range(2):
                        r = slice(64 * h, 64 * h + 64)
                        q = qk[parity][r, n, 0, :]
                        nc.tensor.matmul(S(n, h)[:, 0:REACH], q, qk[1 - parity][r, n, 1, P - REACH:P], start=True, stop=True)
                        last = nc.tensor.matmul(S(n, h)[:, REACH:160], q, qk[parity][r, n, 1, :], start=True, stop=True)
                    last.then_inc(score_product, 1)

                def turn(n):
                    pe.wait_ge(exp_done, PAIRS * g + n + 1 + RAISED)
                    if n == 0:
                        pe.wait_ge(v_copied, g + 1 + RAISED)
                    if n >= 2:
                        pe.wait_ge(pT_copied, PAIRS * g + n - 1 + RAISED)
                    for h in range(2):
                        for k in range(2):
                            last = nc.tensor.transpose(PT(n)[:, h, k, :], probs[n % 2][:, h, k * P:k * P + P], m.ident)
                    last.then_inc(pT_ready, 1)

                def weigh(n):
                    pe.wait_ge(pT_copied, PAIRS * g + n + 1 + RAISED)
                    if n >= 2:
                        pe.wait_ge(ctx_copied, PAIRS * g + n - 1 + RAISED)
                    for h in range(2):
                        nc.tensor.matmul(CTX(n)[:, h, :], probsT[n % 2][96:P, h, 0, :], v[1 - parity][96:P, 2 * n + h, :],
                                         start=True, stop=False)
                        last = nc.tensor.matmul(CTX(n)[:, h, :], probsT[n % 2][:, h, 1, :], v[parity][:, 2 * n + h, :],
                                                start=False, stop=True)
                    last.then_inc(pv_done, 1)

                project(0)
                values()
                norm2(0)
                project(1)
                norm2(1)
                for n in range(PAIRS + 2):
                    if n < PAIRS:
                        score(n)
                    if 1 <= n <= PAIRS:
                        turn(n - 1)
                    if n >= 2:
                        weigh(n - 2)
                pe.wait_ge(ctx_copied, PAIRS * g + PAIRS + RAISED)
                for c in range(8):
                    last = nc.tensor.transpose(CT[:, c, :], context[:, c * P:c * P + P], m.ident)
                last.then_inc(ctxT_ready, 1)
                pe.wait_ge(ctxT_copied, g + 1 + RAISED)
                for c in range(8):
                    last = nc.tensor.matmul(OUT, w("out", c * P, P), contextT[:, c, :], start=(c == 0), stop=(c == 7))
                last.then_inc(out_product, 1)
            pe.wait_ge(ones_ready, 2 + RAISED)
            tiles(pe, tile)

        @block.scalar
        def _(act):
            def tile(b, t2, parity, g):
                def square(j):
                    act.wait_ge(qk_product, 2 * g + j + 1 + RAISED)
                    act.wait_ge(norm2_product, 2 * g + j + RAISED)
                    nc.scalar.activation(squares, QK[:, :, 0:4:2, :], ACT.Square).then_inc(squared, 1)

                def root(j):
                    act.wait_ge(norm2_product, 2 * g + j + 1 + RAISED)
                    act.wait_ge(qk_ready, 2 * g + RAISED)
                    nc.scalar.activation(norms[j], SS, ACT.Sqrt).then_inc(norm_ready, 1)

                def copy_turned(n):
                    act.wait_ge(pT_ready, PAIRS * g + n + 1 + RAISED)
                    if n >= 2:
                        act.wait_ge(pv_done, PAIRS * g + n - 1 + RAISED)
                    nc.scalar.activation(probsT[n % 2], PT(n), ACT.Copy).then_inc(pT_copied, 1)

                square(0)
                act.wait_ge(v_product, g + 1 + RAISED)
                nc.scalar.activation(v[parity][:, :, 0:64], V, ACT.Copy).then_inc(v_copied, 1)
                root(0)
                square(1)
                root(1)
                for n in range(PAIRS + 1):
                    if n < PAIRS:
                        act.wait_ge(negmax_ready, PAIRS * g + n + 1 + RAISED)
                        if n >= 2:
                            act.wait_ge(pT_ready, PAIRS * g + n - 1 + RAISED)
                        for h in range(2):
                            last = nc.scalar.activation(probs[n % 2][:, h, 96:256], scores[n % 2][:, h, :], ACT.Exp,
                                                        scale=8.0, bias=small[n % 2][:, 2 + h:3 + h])
                        last.then_inc(exp_done, 1)
                    if n >= 1:
                        copy_turned(n - 1)
                act.wait_ge(ctxT_ready, g + 1 + RAISED)
                nc.scalar.activation(contextT, CT, ACT.Copy).then_inc(ctxT_copied, 1)
            tiles(act, tile)

        @block.vector
        def _(dve):
            def tile(b, t2, parity, g):
                t0 = t2 * 256 + parity * P
                dve.wait_ge(pv_done, PAIRS * g + RAISED)
                for half, start in ((slice(0, 64), 1), (slice(64, P), 0)):
                    nc.vector.tensor_copy(xs[half, :], hA[half, bass.ds(b, 1), bass.ds(t0 + start, P)]
                                          .rearrange("p o t -> p (o t)")).then_inc(xs_ready, 1)

                def rope(j):
                    dve.wait_ge(squared, 2 * g + j + 1 + RAISED)
                    dve.wait_ge(qk_ready, 2 * g + RAISED)
                    for k, out in ((0, qk[parity][:, 4 * j:4 * j + 4, :, :]), (1, rotated[j])):
                        for side in range(2):
                            table = tables[:, 2 * side + k:2 * side + k + 1, bass.ds(t0, P)].broadcast_to([P, 4, P])
                            last = nc.vector.tensor_tensor(out[:, :, side, :], QK[:, :, 2 * side + k, :], table, ALU.mult)
                        last.then_inc(rope_product, 1)

                def bound(j):
                    dve.wait_ge(norm_ready, 2 * g + j + 1 + RAISED)
                    nc.vector.tensor_scalar(norms[j], norms[j], 1e-12, None, ALU.max).then_inc(recip_step, 1)
                    dve.wait_ge(recip_step, PER_TILE * g + j + 1 + RAISED)

                def invert(j, chunks):
                    nc.vector.reciprocal(norms[j][:, chunks], norms[j][:, chunks]).then_inc(inv_ready, 1)

                def mask(n):
                    dve.wait_ge(score_product, PAIRS * g + n + 1 + RAISED)
                    if n >= 2:
                        dve.wait_ge(exp_done, PAIRS * g + n - 1 + RAISED)
                    if n == 0 and parity == 0:
                        dve.wait_ge(mask_ready, 2 * b + t2 + 1 + RAISED)
                    hold(dve, dve_passed)
                    for h in range(2):
                        last = nc.vector.tensor_tensor_reduce(scores[n % 2][:, h, :], S(n, h),
                                                              mask_even if parity == 0 else m.masks[:, 160:320],
                                                              1.0, MASKED, ALU.add, ALU.max, small[n % 2][:, h:h + 1])
                    last.then_inc(masked, 1)
                    dve.wait_ge(masked, PAIRS * g + n + 1 + RAISED)
                    nc.vector.tensor_scalar(small[n % 2][:, 2:4], small[n % 2][:, 0:2], -8.0, None,
                                            ALU.mult).then_inc(negmax_ready, 1)

                def normalise(n):
                    dve.wait_ge(pv_done, PAIRS * g + n + 1 + RAISED)
                    if n == 0:
                        dve.wait_ge(ctxT_ready, g + RAISED)
                    nc.vector.reciprocal(small[n % 2][:, 4:6], CTX(n)[:, :, 64]).then_inc(recip_step, 1)
                    dve.wait_ge(recip_step, PER_TILE * g + 2 + n + 1 + RAISED)
                    for h in range(2):
                        last = nc.vector.tensor_scalar(context[:, n * P + 64 * h:n * P + 64 * h + 64], CTX(n)[:, h, 0:64],
                                                       small[n % 2][:, 4 + h:5 + h], None, ALU.mult)
                    last.then_inc(ctx_copied, 1)

                rope(0)
                bound(0)
                invert(0, slice(0, 4))
                rope(1)
                bound(1)
                for n in range(PAIRS + 2):
                    if n < 4:
                        invert(1, slice(n, n + 1))
                    if n < PAIRS:
                        mask(n)
                    if n >= 2:
                        normalise(n - 2)
                dve.wait_ge(out_product, g + 1 + RAISED)
                nc.vector.tensor_tensor(hB[:, bass.ds(b, 1), bass.ds(t0 + 1, P)].rearrange("p o t -> p (o t)"),
                                        hA[:, bass.ds(b, 1), bass.ds(t0 + 1, P)].rearrange("p o t -> p (o t)"),
                                        OUT, ALU.add).then_inc(resid_done, 1)
            PER_TILE = 2 + PAIRS
            for p in range(2):
                nc.vector.memset(v[p][:, :, 64:65], 1.0).then_inc(ones_ready, 1)
            tiles(dve, tile)


def shift_tokens(nc, src, dst):
    with phase(nc, "shifted") as (block, shifted):
        @block.vector
        def _(dve):
            for half, start in ((slice(0, 64), 1), (slice(64, P), 0)):
                nc.vector.tensor_copy(dst[half, :].rearrange("p (b t) -> p b t", b=BATCH), src[half, :, start:start + SEQ])


def gated_feed_forward(nc, m, w, x, resid, out):
    ps = m.psum
    hidden = [m.slab(14), m.slab(15), m.slab(12)]
    gates = m.slab(17).rearrange("p (k t) -> p k t", k=4)
    units = [(b, c) for b in range(BATCH) for c in range(3)]
    with phase(nc, "up_product gelu_done hidden_ready down_product down_added") as (
            block, up_product, gelu_done, hidden_ready, down_product, down_added):
        @block.tensor
        def _(pe):
            def down(b):
                pe.wait_ge(hidden_ready, 3 * b + 3)
                if b >= 2:
                    pe.wait_ge(down_added, b - 1)
                for c in range(3):
                    rows = FF1_ROWS[c]
                    last = nc.tensor.matmul(ps[:, 6 + b % 2, :], w("down", c * P, P, rows), hidden[c][0:rows, cols(b)],
                                            start=(c == 0), stop=(c == 2))
                last.then_inc(down_product, 1)

            for n, (b, c) in enumerate(units):
                if n >= 3:
                    pe.wait_ge(hidden_ready, n - 2)
                rows, bank = FF1_ROWS[c], 2 * (n % 3)
                nc.tensor.matmul(ps[0:rows, bank + 1, :], w("up", (3 + c) * P, rows), x[:, cols(b)], start=True, stop=True)
                nc.tensor.matmul(ps[0:rows, bank, :], w("up", c * P, rows), x[:, cols(b)],
                                 start=True, stop=True).then_inc(up_product, 1)
                if n >= 3 and n % 3 == 1:
                    down(b - 1)
            down(BATCH - 1)

        @block.scalar
        def _(act):
            for n, (b, c) in enumerate(units):
                rows = FF1_ROWS[c]
                act.wait_ge(up_product, n + 1)
                if n >= 4:
                    act.wait_ge(hidden_ready, n - 3)
                nc.scalar.activation(gates[0:rows, n % 4, :], ps[0:rows, 2 * (n % 3) + 1, :], ACT.Gelu,
                                     bias=w("b_up", 3 + c, 1, rows)).then_inc(gelu_done, 1)

        @block.vector
        def _(dve):
            def finish(b):
                dve.wait_ge(down_product, b + 1)
                nc.vector.scalar_tensor_tensor(out=out[:, b, 1:PADSEQ], in0=ps[:, 6 + b % 2, :], scalar=w("b_down"),
                                               in1=resid[:, b, 1:PADSEQ], op0=ALU.add, op1=ALU.add).then_inc(down_added, 1)

            for n, (b, c) in enumerate(units):
                rows = FF1_ROWS[c]
                dve.wait_ge(gelu_done, n + 1)
                nc.vector.scalar_tensor_tensor(out=hidden[c][0:rows, cols(b)], in0=ps[0:rows, 2 * (n % 3), :],
                                               scalar=w("b_up", c, 1, rows), in1=gates[0:rows, n % 4, :],
                                               op0=ALU.add, op1=ALU.mult).then_inc(hidden_ready, 1)
                if n >= 3 and c == 2:
                    finish(b - 1)
            finish(BATCH - 1)


MIX = 32
DECAY = 64
HD_R = 64
R_PARTS = [("tm_w1", 5 * MIX), ("tm_w2", P), ("tm_w2_last", P), ("td_w1", DECAY), ("td_w2", P), ("Wr", P), ("Wk", P),
           ("Wv", P), ("Wg", P), ("Wo", P), ("cWk", 3 * P), ("cWv", 3 * P), ("cWr", P), ("ln1_w", 1), ("ln2_w", 1),
           ("x_maa", 1), ("w_maa", 1), ("k_maa", 1), ("v_maa", 1), ("r_maa", 1), ("g_maa", 1), ("time_decay", 1),
           ("time_first", 1), ("gn_w", 1), ("gn_b", 1), ("ck_maa", 1), ("cr_maa", 1), ("ln_out_w", 1)]
SPREAD = HD_R - 1 + P


def by_batch(a):
    return a.rearrange("p (b t) -> p b t", b=BATCH)


def recurrent_network(nc, m, ins, xn, s_out):
    where, width = offsets(R_PARTS)
    W = m.weights[:, 0:width]
    h, y, sx, mixes, mix_last = (m.slab(i) for i in (3, 4, 5, 6, 7))
    decay, k, v, r, gate, out = (m.slab(i) for i in (9, 10, 11, 12, 13, 14))

    def w(name, a=0, n=None, rows=slice(0, P)):
        o, width = where[name]
        return W[rows, o + a:o + (a + n if n else width)]

    with phase(nc, "copied") as (block, copied):
        @block.vector
        def _(dve):
            nc.vector.tensor_copy(h, xn)

    with nc.Fori(0, 2) as layer:
        load(nc, [(W, ins["R"][bass.ds(layer, 1)].rearrange("l p n -> (l p) n"))], "rwkv")
        layer_norm(nc, m, h, y, w("ln1_w"), tag="ln1")
        token_difference(nc, y, sx)
        token_mix(nc, m, w, y, sx, mixes, mix_last, (decay, k, v, r, gate))
        state_scan(nc, m, w, ins, decay, k, v, r, out)
        layer_norm(nc, m, out, out, w("gn_w"), w("gn_b"), tag="gn", mean=m.mean_halves, refine=False)
        time_mix_output(nc, m, w, out, gate, h)
        layer_norm(nc, m, h, y, w("ln2_w"), tag="ln2")
        token_difference(nc, y, sx)
        channel_mix(nc, m, w, y, sx, h)
    layer_norm(nc, m, h, s_out, w("ln_out_w"), tag="lnout")


def token_difference(nc, y, sx):
    with phase(nc, "difference") as (block, difference):
        @block.vector
        def _(dve):
            yb, sb = by_batch(y), by_batch(sx)
            nc.vector.tensor_scalar(sb[:, :, 0:1], yb[:, :, 0:1], -1.0, None, ALU.mult)
            for b in range(BATCH):
                nc.vector.tensor_tensor(sb[:, b, 1:SEQ], yb[:, b, 0:SEQ - 1], yb[:, b, 1:SEQ], ALU.subtract)


def token_mix(nc, m, w, y, sx, mixes, mix_last, outs):
    ps = m.psum
    xxx = m.slab(8)
    with phase(nc, "xxx_ready mix_product mix_done") as (block, xxx_ready, mix_product, mix_done):
        @block.vector
        def _(dve):
            for b in range(BATCH):
                nc.vector.scalar_tensor_tensor(out=xxx[:, cols(b)], in0=sx[:, cols(b)], scalar=w("x_maa"),
                                               in1=y[:, cols(b)], op0=ALU.mult, op1=ALU.add).then_inc(xxx_ready, 1)

        @block.tensor
        def _(pe):
            for b in range(BATCH):
                pe.wait_ge(xxx_ready, b + 1)
                nc.tensor.matmul(ps[:, 2 * b, :], w("tm_w1", 0, 4 * MIX), xxx[:, cols(b)], start=True, stop=True)
                nc.tensor.matmul(ps[0:MIX, 2 * b + 1, :], w("tm_w1", 4 * MIX, MIX), xxx[:, cols(b)],
                                 start=True, stop=True).then_inc(mix_product, 1)

        @block.scalar
        def _(act):
            for b in range(BATCH):
                act.wait_ge(mix_product, b + 1)
                nc.scalar.activation(mixes[:, cols(b)], ps[:, 2 * b, :], ACT.Tanh)
                nc.scalar.activation(mix_last[0:MIX, cols(b)], ps[0:MIX, 2 * b + 1, :], ACT.Tanh).then_inc(mix_done, 1)

    decay, k, v, r, gate = outs
    names = ["w_maa", "k_maa", "v_maa", "r_maa", "g_maa"]
    mixed = [m.slab(15), m.slab(16)]
    units = [(f, b) for f in range(5) for b in range(BATCH)]
    low = m.slab(17)
    with phase(nc, "shift_product scaled mixed_ready projected done low_product low_done decay_product decay_exp decay_tanh decay_step") as (
            block, shift_product, scaled, mixed_ready, projected, done, low_product, low_done, decay_product, decay_exp, decay_tanh,
            decay_step):
        @block.tensor
        def _(pe):
            def project(n):
                f, b = units[n]
                pe.wait_ge(mixed_ready, n + 1)
                if n >= 4:
                    pe.wait_ge(done, n - 3)
                x = mixed[f % 2][:, cols(b)]
                if f == 0:
                    out, weight = ps[0:DECAY, 4 + n % 4, :], w("td_w1")
                else:
                    out, weight = ps[:, 4 + n % 4, :], w(["Wk", "Wv", "Wr", "Wg"][f - 1])
                nc.tensor.matmul(out, weight, x, start=True, stop=True).then_inc(projected, 1)

            for n, (f, b) in enumerate(units):
                if n >= 4:
                    pe.wait_ge(scaled, n - 3)
                rows = slice(MIX * f, MIX * f + MIX) if f < 4 else slice(0, MIX)
                weight = w("tm_w2" if f < 4 else "tm_w2_last", rows=rows)
                src = (mixes if f < 4 else mix_last)[rows, cols(b)]
                nc.tensor.matmul(ps[:, n % 4, :], weight, src, start=True, stop=True).then_inc(shift_product, 1)
                if n >= 2:
                    project(n - 2)
            project(18)
            project(19)
            for b in range(BATCH):
                pe.wait_ge(done, 20)
                nc.tensor.matmul(ps[:, b, :], w("td_w2", rows=slice(0, DECAY)), low[0:DECAY, cols(b)],
                                 start=True, stop=True).then_inc(decay_product, 1)

        @block.vector
        def _(dve):
            for n, (f, b) in enumerate(units):
                dve.wait_ge(shift_product, n + 1)
                if n >= 8:
                    dve.wait_ge(projected, n - 7)
                x = mixed[f % 2][:, cols(b)]
                nc.vector.scalar_tensor_tensor(out=x, in0=ps[:, n % 4, :], scalar=w(names[f]),
                                               in1=sx[:, cols(b)], op0=ALU.add, op1=ALU.mult).then_inc(scaled, 1)
            for b in range(BATCH):
                dve.wait_ge(done, 16 + b + 1)
                nc.vector.scalar_tensor_tensor(out=gate[:, cols(b)], in0=gate[:, cols(b)], scalar=1.0, in1=ps[:, 4 + b, :],
                                               op0=ALU.add, op1=ALU.mult)
            for b in range(BATCH):
                nc.vector.tensor_scalar(r[:, cols(b)], r[:, cols(b)], 0.5, 0.5, ALU.mult, ALU.add)
            link = Chain(dve, decay_step)
            inv = m.slab(15)[:, 0:SEQ]
            dve.wait_ge(projected, len(units))
            for b in range(BATCH):
                d = decay[:, cols(b)]
                dve.wait_ge(decay_tanh, b + 1)
                link(nc.vector.tensor_scalar(inv, d, -1.0, 1.0, ALU.mult, ALU.add))
                link(nc.vector.reciprocal(inv, inv))
                link(nc.vector.tensor_tensor(d, d, inv, ALU.mult))
                link(nc.vector.tensor_scalar(d, d, 2.0, 1.0, ALU.mult, ALU.add))

        @block.gpsimd
        def _(pool):
            for n, (f, b) in enumerate(units):
                x = mixed[f % 2][:, cols(b)]
                pool.wait_ge(scaled, n + 1)
                nc.gpsimd.tensor_tensor(x, x, y[:, cols(b)], ALU.add).then_inc(mixed_ready, 1)

        @block.scalar
        def _(act):
            for n, (f, b) in enumerate(units):
                act.wait_ge(projected, n + 1)
                func = [ACT.Tanh, ACT.Copy, ACT.Copy, ACT.Tanh, ACT.Tanh][f]
                rows = DECAY if f == 0 else P
                dst = [low, k, v, r, gate][f]
                nc.scalar.activation(dst[0:rows, cols(b)], ps[0:rows, 4 + n % 4, :], func,
                                     scale=0.5 if f >= 3 else 1.0).then_inc(done, 1)
            for b in range(BATCH):
                act.wait_ge(decay_product, b + 1)
                nc.scalar.activation(decay[:, cols(b)], ps[:, b, :], ACT.Exp, bias=w("time_decay")).then_inc(decay_exp, 1)
            for b in range(BATCH):
                act.wait_ge(decay_exp, b + 1)
                nc.scalar.activation(decay[:, cols(b)], decay[:, cols(b)], ACT.Tanh, scale=-0.5).then_inc(decay_tanh, 1)


def state_scan(nc, m, w, ins, decay, k, v, r, out):
    ps = m.psum
    spread = m.slab(15)[:, 0:192]
    pick = [m.slab(15)[:, 256 + P * p:256 + P * p + P] for p in range(2)]
    gather = [m.slab(15)[:, 512 + P * p:512 + P * p + P] for p in range(2)]
    zeros = m.slab(15)[:, 768:768 + P]
    fed = [m.slab(16)[:, 512 * p:512 * p + 512] for p in range(2)]
    read = [m.slab(16)[:, 1024 + 512 * p:1536 + 512 * p] for p in range(2)]
    state = [m.slab(17, 2)[:, 520 * p:520 * p + SEQ + 1] for p in range(2)]
    bonus = m.slab(8)
    ident2 = m.ident.rearrange("p (h j) -> p h j", h=2)
    JOBS = HD_R
    load(nc, [(spread, ins["spread"])], "spread")
    with phase(nc, "zeroed selected spread_product fed_ready state_ready read_ready gathered "
                   "finished bonus_ready bonus_product own", raised=True) as (
            block, zeroed, selected, spread_product, fed_ready, state_ready, read_ready, gathered,
            finished, bonus_ready, bonus_product, own):
        @block.scalar
        def _(act):
            with act.Fori(0, JOBS // 2) as jj:
                for p in range(2):
                    j = jj * 2 + p
                    act.wait_ge(gathered, 4 * j + RAISED)
                    src = ident2[:, :, bass.ds(j, 1)].broadcast_to([P, 2, 64])
                    nc.scalar.activation(pick[p].rearrange("p (h j) -> p h j", h=2), src, ACT.Copy).then_inc(selected, 1)
                    nc.scalar.activation(gather[p], spread[:, bass.ds(63 - j, P)], ACT.Copy).then_inc(selected, 1)

        @block.tensor
        def _(pe):
            def spread_row(j, p, b, first=False):
                if b == 0:
                    pe.wait_ge(selected, 2 * j + 2 + RAISED)
                if not first:
                    pe.wait_ge(fed_ready, 4 * j + b - 3 + RAISED)
                nc.tensor.matmul(ps[:, 4 + b, :], pick[p], v[:, cols(b)], start=True, stop=True).then_inc(spread_product, 1)

            def sum_keys(j, p, b):
                pe.wait_ge(read_ready, 4 * j + b + 1 + RAISED)
                nc.tensor.matmul(ps[:, b, :], gather[p], read[b % 2], start=False, stop=False,
                                 skip_group_check=True).then_inc(gathered, 1)

            pe.wait_ge(zeroed, 1 + RAISED)
            for b in range(BATCH):
                nc.tensor.matmul(ps[:, b, :], zeros, v[:, cols(b)], start=True, stop=False,
                                 skip_group_check=True).then_inc(gathered, 1)
            for b in range(BATCH):
                spread_row(0, 0, b, first=True)
            with pe.Fori(0, JOBS // 2 - 1) as jj:
                for p in range(2):
                    for b in range(BATCH):
                        sum_keys(jj * 2 + p, p, b)
                        spread_row(jj * 2 + p + 1, 1 - p, b)
            for b in range(BATCH):
                sum_keys(JOBS - 2, 0, b)
                spread_row(JOBS - 1, 1, b)
            for b in range(BATCH):
                sum_keys(JOBS - 1, 1, b)
            for b in range(BATCH):
                nc.tensor.matmul(ps[:, b, :], zeros, v[:, cols(b)], start=False, stop=True,
                                 skip_group_check=True).then_inc(finished, 1)
            for b in range(BATCH):
                pe.wait_ge(bonus_ready, b + 1 + RAISED)
                nc.tensor.matmul(ps[:, 4 + b, :], m.halves, bonus[:, cols(b)], start=True, stop=True).then_inc(bonus_product, 1)

        @block.vector
        def _(dve):
            nc.vector.memset(zeros, 0.0).then_inc(zeroed, 1)
            for b in range(BATCH):
                nc.vector.scalar_tensor_tensor(out=bonus[:, cols(b)], in0=r[:, cols(b)], scalar=w("time_first"),
                                               in1=k[:, cols(b)], op0=ALU.mult, op1=ALU.mult).then_inc(bonus_ready, 1)
            for p in range(2):
                nc.vector.memset(state[p][:, 0:1], 0.0)
            with dve.Fori(0, JOBS) as j:
                for b in range(BATCH):
                    dve.wait_ge(spread_product, 4 * j + b + 1 + RAISED)
                    nc.vector.tensor_tensor(fed[b % 2], k[:, cols(b)], ps[:, 4 + b, :], ALU.mult).then_inc(fed_ready, 1)
                    dve.wait_ge(fed_ready, 4 * j + b + 1 + RAISED)
                    if b >= 2:
                        dve.wait_ge(read_ready, 4 * j + b - 1 + RAISED)
                    else:
                        dve.wait_ge(read_ready, 4 * j + RAISED)
                    nc.vector.tensor_tensor_scan(state[b % 2][:, 1:SEQ + 1], decay[:, cols(b)], fed[b % 2], 0.0,
                                                 ALU.mult, ALU.add).then_inc(state_ready, 1)
            link = Chain(dve, own, RAISED)
            for b in range(BATCH):
                dve.wait_ge(bonus_product, b + 1 + RAISED)
                dve.wait_ge(finished, b + 1 + RAISED)
                o = out[:, cols(b)]
                link(nc.vector.tensor_tensor(o, v[:, cols(b)], ps[:, 4 + b, :], ALU.mult))
                link(nc.vector.tensor_tensor(o, o, ps[:, b, :], ALU.add))

        @block.gpsimd
        def _(pool):
            with pool.Fori(0, JOBS) as j:
                for b in range(BATCH):
                    pool.wait_ge(state_ready, 4 * j + b + 1 + RAISED)
                    pool.wait_ge(gathered, 4 * j + b + 3 + RAISED)
                    nc.gpsimd.tensor_tensor(read[b % 2], r[:, cols(b)], state[b % 2][:, 0:SEQ], ALU.mult).then_inc(read_ready, 1)


def time_mix_output(nc, m, w, out, gate, h):
    ps = m.psum
    with phase(nc, "gated wo_product") as (block, gated, wo_product):
        @block.gpsimd
        def _(pool):
            for b in range(BATCH):
                nc.gpsimd.tensor_tensor(out[:, cols(b)], out[:, cols(b)], gate[:, cols(b)], ALU.mult).then_inc(gated, 1)

        @block.tensor
        def _(pe):
            for b in range(BATCH):
                pe.wait_ge(gated, b + 1)
                nc.tensor.matmul(ps[:, b, :], w("Wo"), out[:, cols(b)], start=True, stop=True).then_inc(wo_product, 1)

        @block.vector
        def _(dve):
            for b in range(BATCH):
                dve.wait_ge(wo_product, b + 1)
                nc.vector.scalar_tensor_tensor(out=h[:, cols(b)], in0=ps[:, b, :], scalar=0.5, in1=h[:, cols(b)],
                                               op0=ALU.mult, op1=ALU.add)


def channel_mix(nc, m, w, y, sx, h):
    ps = m.psum
    kx, rx, sig = m.slab(6), m.slab(7), m.slab(8)
    hidden = [m.slab(9 + c) for c in range(3)]
    with phase(nc, "kx_ready rx_ready key_product relu_done hidden_ready receptance_product sig_ready value_product own") as (
            block, kx_ready, rx_ready, key_product, relu_done, hidden_ready, receptance_product, sig_ready, value_product, own):
        @block.vector
        def _(dve):
            for x, maa, ready in ((kx, "ck_maa", kx_ready), (rx, "cr_maa", rx_ready)):
                for b in range(BATCH):
                    nc.vector.scalar_tensor_tensor(out=x[:, cols(b)], in0=sx[:, cols(b)], scalar=w(maa),
                                                   in1=y[:, cols(b)], op0=ALU.mult, op1=ALU.add).then_inc(ready, 1)
            link = Chain(dve, own)
            for b in range(BATCH):
                dve.wait_ge(value_product, b + 1)
                dve.wait_ge(sig_ready, b + 1)
                link(nc.vector.scalar_tensor_tensor(out=sig[:, cols(b)], in0=sig[:, cols(b)], scalar=1.0, in1=ps[:, 6 + b % 2, :],
                                                    op0=ALU.add, op1=ALU.mult))
                link(nc.vector.scalar_tensor_tensor(out=h[:, cols(b)], in0=sig[:, cols(b)], scalar=0.5, in1=h[:, cols(b)],
                                                    op0=ALU.mult, op1=ALU.add))

        @block.tensor
        def _(pe):
            def value(b):
                pe.wait_ge(hidden_ready, 3 * b + 3)
                if b >= 2:
                    pe.wait_ge(own, 2 * (b - 1))
                for c in range(3):
                    last = nc.tensor.matmul(ps[:, 6 + b % 2, :], w("cWv", c * P, P), hidden[c][:, cols(b)],
                                            start=(c == 0), stop=(c == 2))
                last.then_inc(value_product, 1)

            for b in range(BATCH):
                pe.wait_ge(kx_ready, b + 1)
                for c in range(3):
                    n = 3 * b + c
                    if n >= 4:
                        pe.wait_ge(relu_done, n - 3)
                    nc.tensor.matmul(ps[:, n % 4, :], w("cWk", c * P, P), kx[:, cols(b)], start=True, stop=True).then_inc(key_product, 1)
            for b in range(BATCH):
                pe.wait_ge(rx_ready, b + 1)
                if b >= 2:
                    pe.wait_ge(sig_ready, b - 1)
                nc.tensor.matmul(ps[:, 4 + b % 2, :], w("cWr"), rx[:, cols(b)], start=True, stop=True).then_inc(receptance_product, 1)
            for b in range(BATCH):
                value(b)

        @block.scalar
        def _(act):
            for n in range(12):
                b, c = n // 3, n % 3
                act.wait_ge(key_product, n + 1)
                nc.scalar.activation(hidden[c][:, cols(b)], ps[:, n % 4, :], ACT.Relu).then_inc(relu_done, 1)
                act.wait_ge(relu_done, n + 1)
                nc.scalar.activation(hidden[c][:, cols(b)], hidden[c][:, cols(b)], ACT.Square).then_inc(hidden_ready, 1)
            for b in range(BATCH):
                act.wait_ge(receptance_product, b + 1)
                nc.scalar.activation(sig[:, cols(b)], ps[:, 4 + b % 2, :], ACT.Tanh, scale=0.5).then_inc(sig_ready, 1)


TOPK = 31
A_PARTS = [("q2", 4 * P), ("k2", 4 * P), ("v2", P), ("o2", P), ("v_row2", P), ("bq2", 4), ("bk2", 4), ("bo2", 1)]


def full_attention(nc, m, xn, out, weights, heads, scale, top, mask=None):
    ps = m.psum
    w = weights
    dh, groups = P // heads, heads // 4
    keys = m.slab(6)[:, 0:groups * SEQ].rearrange("p (g t) -> p g t", g=groups)
    v = m.slab(7)[:, 0:4 * heads * (dh + 1)].rearrange("p (t h d) -> p t h d", t=4, h=heads)
    xb = m.slab(8)[:, 0:SEQ]
    q = m.slab(8)[:, SEQ:SEQ + groups * P].rearrange("p (g t) -> p g t", g=groups)
    ctx = m.slab(8)[:, 1024:1024 + P]
    ctxT = m.slab(8)[:, 1152:1280]
    inv = m.slab(8)[:, 1280:1280 + heads]
    final = m.slab(8)[:, 1408:1408 + P]
    scores = [m.slab(9)[:, 512 * n:512 * n + 512] for n in range(4)]
    work = [m.slab(10)[:, 512 * n:512 * n + 512] for n in range(2)]
    tops = [m.slab(8)[:, 1536 + 40 * n:1576 + 40 * n] for n in range(4)]
    probs = [m.slab(11)[:, 512 * n:512 * n + 512] for n in range(4)]
    kept = [m.slab(12)[:, 512 * n:512 * n + 512] for n in range(2)]
    probsT = [m.slab(13)[:, 512 * n:512 * n + 512].rearrange("p (k q) -> p k q", k=4) for n in range(2)]
    CTX = ps[:, 6, 0:heads * (dh + 1)].rearrange("p (h d) -> p h d", h=heads)

    with nc.Fori(0, BATCH) as batch:
        with phase(nc, "x_staged key_product keys_done value_product ones_set") as (
                block, x_staged, key_product, keys_done, value_product, ones_set):
            @block.vector
            def _(dve):
                nc.vector.tensor_copy(xb, xn[:, bass.ds(batch * SEQ, SEQ)]).then_inc(x_staged, 1)
                nc.vector.memset(v[:, :, :, dh:dh + 1], 1.0)
                for t in range(4):
                    dve.wait_ge(value_product, t + 1)
                    nc.vector.tensor_copy(v[:, t, :, 0:dh], ps[:, 4 + t, 0:P].rearrange("p (h d) -> p h d", h=heads))

            @block.tensor
            def _(pe):
                pe.wait_ge(x_staged, 1)
                for c in range(groups):
                    nc.tensor.matmul(ps[:, c, :], w["k"](c), xb, start=True, stop=True).then_inc(key_product, 1)
                for t in range(4):
                    nc.tensor.matmul(ps[:, 4 + t, 0:P], xb[:, t * P:t * P + P], w["v"], start=True, stop=False)
                    nc.tensor.matmul(ps[:, 4 + t, 0:P], m.ones_row, w["v_row"],
                                     start=False, stop=True).then_inc(value_product, 1)

            @block.scalar
            def _(act):
                for c in range(groups):
                    act.wait_ge(key_product, c + 1)
                    nc.scalar.activation(keys[:, c, :], ps[:, c, :], ACT.Identity, bias=w["bk"](c))

        with phase(nc, "q_product q_ready score_product scores_copied picked negmax_ready exp_done kept_ready probs_ready "
                       "pT_ready pT_copied pv_done ctx_ready ctxT_product ctxT_copied out_product out_done top_step norm_step "
                       "dve_passed pool_passed", raised=True) as (
                block, q_product, q_ready, score_product, scores_copied, picked, negmax_ready, exp_done, kept_ready, probs_ready,
                pT_ready, pT_copied, pv_done, ctx_ready, ctxT_product, ctxT_copied, out_product, out_done, top_step, norm_step,
                dve_passed, pool_passed):
            @block.tensor
            def _(pe):
                with pe.Fori(0, 4) as t:
                    u0 = t * heads
                    pe.wait_ge(out_done, t + RAISED)
                    for c in range(groups):
                        last = nc.tensor.matmul(ps[:, 7, c * P:c * P + P], w["q"](c), xn[:, bass.ds(batch * SEQ + t * P, P)],
                                                start=True, stop=True)
                    last.then_inc(q_product, 1)
                    pe.wait_ge(q_ready, groups * (t + 1) + RAISED)

                    def score(n):
                        if n < 4:
                            pe.wait_ge(scores_copied, u0 + RAISED)
                        else:
                            pe.wait_ge(scores_copied, u0 + n - 3 + RAISED)
                        rows = slice(32 * (n % 4), 32 * (n % 4) + dh)
                        nc.tensor.matmul(ps[:, n % 4, :], q[rows, n // 4, :], keys[rows, n // 4, :],
                                         start=True, stop=True).then_inc(score_product, 1)

                    def turn(n):
                        pe.wait_ge(probs_ready, u0 + n + 1 + RAISED)
                        if n >= 2:
                            pe.wait_ge(pT_copied, u0 + n - 1 + RAISED)
                        for k in range(4):
                            last = nc.tensor.transpose(ps[:, 4 + n % 2, k * P:k * P + P], probs[n % 4][:, k * P:k * P + P], m.ident)
                        last.then_inc(pT_ready, 1)

                    def weigh(n):
                        pe.wait_ge(pT_copied, u0 + n + 1 + RAISED)
                        for k in range(4):
                            last = nc.tensor.matmul(CTX[:, n, :], probsT[n % 2][:, k, :], v[:, k, n, :], start=(k == 0), stop=(k == 3))
                        last.then_inc(pv_done, 1)

                    for n in range(heads + 3):
                        if n < heads:
                            score(n)
                        if 2 <= n < heads + 2:
                            turn(n - 2)
                        if n >= 3:
                            weigh(n - 3)
                    pe.wait_ge(ctx_ready, t + 1 + RAISED)
                    nc.tensor.transpose(ps[:, 7, 0:P], ctx, m.ident).then_inc(ctxT_product, 1)
                    pe.wait_ge(ctxT_copied, t + 1 + RAISED)
                    nc.tensor.matmul(ps[:, 7, 0:P], w["o"], ctxT, start=True, stop=True).then_inc(out_product, 1)

            @block.scalar
            def _(act):
                with act.Fori(0, 4) as t:
                    u0 = t * heads

                    def copy_turned(n):
                        act.wait_ge(pT_ready, u0 + n + 1 + RAISED)
                        if n >= 2:
                            act.wait_ge(pv_done, u0 + n - 1 + RAISED)
                        nc.scalar.activation(probsT[n % 2], ps[:, 4 + n % 2, :].rearrange("p (k q) -> p k q", k=4),
                                             ACT.Copy).then_inc(pT_copied, 1)

                    def copy_scores(n):
                        act.wait_ge(score_product, u0 + n + 1 + RAISED)
                        if n >= 4:
                            act.wait_ge(kept_ready if top else probs_ready, u0 + n - 3)
                        nc.scalar.activation(scores[n % 4], ps[:, n % 4, :], ACT.Copy).then_inc(scores_copied, 1)

                    def exponential(n):
                        act.wait_ge(negmax_ready, u0 + n + 1 + RAISED)
                        if n >= 4:
                            act.wait_ge(pT_ready, u0 + n - 3 + RAISED)
                        if top:
                            nc.scalar.activation(probs[n % 4], scores[n % 4], ACT.Exp, bias=tops[n % 4][:, 32:33],
                                                 scale=scale).then_inc(exp_done, 1)
                        else:
                            nc.scalar.activation(probs[n % 4], scores[n % 4], ACT.Exp, bias=tops[n % 4][:, 32:33],
                                                 scale=scale).then_inc(probs_ready, 1)

                    for n in range(heads + 3):
                        if n < heads:
                            copy_scores(n)
                        if 1 <= n <= heads:
                            exponential(n - 1)
                        if n >= 3:
                            copy_turned(n - 3)
                    act.wait_ge(ctxT_product, t + 1 + RAISED)
                    if mask is None:
                        nc.scalar.activation(ctxT, ps[:, 7, 0:P], ACT.Copy).then_inc(ctxT_copied, 1)

            @block.vector
            def _(dve):
                with dve.Fori(0, 4) as t:
                    u0 = t * heads
                    dve.wait_ge(q_product, t + 1 + RAISED)
                    for c in range(groups):
                        nc.vector.tensor_scalar(q[:, c, :], ps[:, 7, c * P:c * P + P], w["bq"](c), None, ALU.add).then_inc(q_ready, 1)
                    steps = 7 if top else 1
                    for n in range(heads):
                        mx, s, wk = tops[n % 4], scores[n % 4], work[n % 2]
                        dve.wait_ge(scores_copied, u0 + n + 1 + RAISED)
                        if n >= 4:
                            dve.wait_ge(exp_done if top else probs_ready, u0 + n - 3)
                        hold(dve, dve_passed)
                        link = Chain(dve, top_step, (u0 + n) * steps + RAISED, dve_passed)
                        link(nc.vector.max(mx[:, 0:8], s))
                        if top:
                            for k in range(1, 4):
                                link(nc.vector.match_replace(out=wk, in_to_replace=mx[:, 8 * k - 8:8 * k],
                                                             in_values=s if k == 1 else wk, imm_value=MASKED))
                                link(nc.vector.max(mx[:, 8 * k:8 * k + 8], wk))
                        nc.vector.tensor_scalar(mx[:, 32:33], mx[:, 0:1], -scale, None, ALU.mult).then_inc(negmax_ready, 1)
                    dve.wait_ge(pv_done, u0 + heads + RAISED)
                    dve.wait_ge(ctxT_product, t + RAISED)
                    link = Chain(dve, norm_step, t + RAISED)
                    link(nc.vector.reciprocal(inv, CTX[:, :, dh]))
                    nc.vector.tensor_tensor(ctx.rearrange("p (h d) -> p h d", h=heads), CTX[:, :, 0:dh],
                                            inv.rearrange("p (h o) -> p h o", o=1).broadcast_to([P, heads, dh]),
                                            ALU.mult).then_inc(ctx_ready, 1)
                    if mask is not None:
                        dve.wait_ge(ctxT_product, t + 1 + RAISED)
                        nc.vector.tensor_tensor(ctxT, ps[:, 7, 0:P], mask[:, bass.ds(t * P, P)], ALU.mult).then_inc(ctxT_copied, 1)
                    dve.wait_ge(out_product, t + 1 + RAISED)
                    o = out[:, bass.ds(batch * SEQ + t * P, P)]
                    if mask is None:
                        nc.vector.tensor_scalar(o, ps[:, 7, 0:P], w["bo"], None, ALU.add).then_inc(out_done, 1)
                    else:
                        nc.vector.scalar_tensor_tensor(out=o, in0=ps[:, 7, 0:P], scalar=w["bo"], in1=mask[:, bass.ds(t * P, P)],
                                                       op0=ALU.add, op1=ALU.mult).then_inc(out_done, 1)

            if top:
                @block.gpsimd
                def _(pool):
                    with pool.Fori(0, 4) as t:
                        u0 = t * heads
                        for n in range(heads):
                            pool.wait_ge(negmax_ready, u0 + n + 1 + RAISED)
                            hold(pool, pool_passed)
                            nc.gpsimd.tensor_scalar(kept[n % 2], scores[n % 4], tops[n % 4][:, TOPK - 1:TOPK], None,
                                                    ALU.is_ge).then_inc(kept_ready, 1)
                            pool.wait_ge(kept_ready, u0 + n + 1 + RAISED)
                            pool.wait_ge(exp_done, u0 + n + 1 + RAISED)
                            nc.gpsimd.tensor_tensor(probs[n % 4], probs[n % 4], kept[n % 2], ALU.mult).then_inc(probs_ready, 1)


EXPERTS, GROUPS, PICKED_GROUPS, PICKED = 16, 4, 2, 4
M_PARTS = [("router", EXPERTS), ("gate", 8 * P), ("up", 8 * P), ("down", 8 * P), ("rows", 8 * P), ("e_bias", TOK // P * EXPERTS)]


def experts(nc, m, w, xn, g_out):
    ps = m.psum
    tiles, n = TOK // P, TOK // P * EXPERTS
    area = m.slab(6)
    sc, choice, cmp, rank, other = (area[:, 256 * i:256 * i + 256].rearrange("p (t e) -> p t e", e=EXPERTS) for i in range(5))
    pair, gsum, grank, gcmp = (area[:, 1280 + 64 * i:1344 + 64 * i].rearrange("p (t g) -> p t g", g=GROUPS) for i in range(4))
    denom = area[:, 1600:1616]
    combineT = m.slab(7)
    with phase(nc, "logits_ready sig_ready route_step turned combineT_done") as (
            block, logits_ready, sig_ready, route_step, turned, combineT_done):
        @block.tensor
        def _(pe):
            for t in range(tiles):
                last = nc.tensor.matmul(ps[:, 0, t * EXPERTS:t * EXPERTS + EXPERTS], xn[:, t * P:t * P + P], w("router"),
                                        start=True, stop=True)
            last.then_inc(logits_ready, 1)
            pe.wait_ge(turned, 1)
            for t in range(tiles):
                last = nc.tensor.transpose(ps[0:EXPERTS, 4 + t // 4, (t % 4) * P:(t % 4) * P + P], choice[:, t, :], m.ident)
            last.then_inc(turned, 1)

        @block.scalar
        def _(act):
            act.wait_ge(logits_ready, 1)
            nc.scalar.activation(sc, ps[:, 0, 0:n].rearrange("p (t e) -> p t e", e=EXPERTS), ACT.Sigmoid).then_inc(sig_ready, 1)
            act.wait_ge(turned, 2)
            for b in range(BATCH):
                nc.scalar.activation(combineT[0:EXPERTS, cols(b)], ps[0:EXPERTS, 4 + b, :], ACT.Copy)

        @block.vector
        def _(dve):
            link = Chain(dve, route_step)
            v = nc.vector
            dve.wait_ge(sig_ready, 1)
            link(v.tensor_tensor(choice, sc, w("e_bias").rearrange("p (t e) -> p t e", e=EXPERTS), ALU.add))
            c4 = choice.rearrange("p t (g k) -> p t g k", k=4)
            pairs = [(i, j) for i in range(4) for j in range(i + 1, 4)]
            for q, (i, j) in enumerate(pairs):
                dst = gsum if q == 0 else pair
                link(v.tensor_tensor(dst, c4[:, :, :, i], c4[:, :, :, j], ALU.add))
                if q:
                    link(v.tensor_tensor(gsum, gsum, pair, ALU.max))
            link(v.memset(grank, 0.0))
            rank_before(link, v, grank, gsum, gcmp, GROUPS)
            link(v.tensor_scalar(gcmp, grank, PICKED_GROUPS - 0.5, None, ALU.is_lt))
            mask = gcmp.rearrange("p t (g o) -> p t g o", o=1).broadcast_to([P, tiles, GROUPS, 4])
            link(v.tensor_tensor(other.rearrange("p t (g k) -> p t g k", k=4), c4, mask, ALU.mult))
            link(v.memset(rank, 0.0))
            rank_before(link, v, rank, other, cmp, EXPERTS)
            link(v.tensor_scalar(cmp, rank, PICKED - 0.5, None, ALU.is_lt))
            link(v.tensor_tensor(sc, sc, cmp, ALU.mult))
            link(v.reduce_sum(denom, sc, axis=AX.X))
            link(v.tensor_scalar(denom, denom, 1e-20, None, ALU.add))
            link(v.reciprocal(denom, denom))
            link(v.tensor_tensor(choice, sc, denom.rearrange("p (t o) -> p t o", o=1).broadcast_to([P, tiles, EXPERTS]), ALU.mult))
            v.memset(area[:, 1700:1701], 0.0).then_inc(turned, 1)

    acts = [m.slab(8)[:, 512 * i:512 * i + 512] for i in range(4)]
    units = [(b, c) for b in range(BATCH) for c in range(8)]
    with phase(nc, "expert_product silu_done act_step act_ready down_product down_copied") as (
            block, expert_product, silu_done, act_step, act_ready, down_product, down_copied):
        @block.tensor
        def _(pe):
            def down(n):
                b, c = units[n]
                pe.wait_ge(act_ready, n + 1)
                if b >= 2 and c == 0:
                    pe.wait_ge(down_copied, b - 1)
                last = nc.tensor.matmul(ps[:, 6 + b % 2, :], w("down", c * P, P), acts[n % 4], start=(c == 0), stop=(c == 7))
                last.then_inc(down_product, 1)

            for n, (b, c) in enumerate(units):
                if n >= 2:
                    pe.wait_ge(act_ready, n - 1)
                bank = 3 * (n % 2)
                nc.tensor.matmul(ps[:, bank, :], w("gate", c * P, P), xn[:, cols(b)], start=True, stop=True)
                nc.tensor.matmul(ps[:, bank + 1, :], w("up", c * P, P), xn[:, cols(b)], start=True, stop=True)
                nc.tensor.matmul(ps[:, bank + 2, :], w("rows", c * P, P)[0:EXPERTS, :], combineT[0:EXPERTS, cols(b)],
                                 start=True, stop=True).then_inc(expert_product, 1)
                if n >= 1:
                    down(n - 1)
            down(len(units) - 1)

        @block.scalar
        def _(act):
            def store(b):
                act.wait_ge(down_product, 8 * b + 8)
                nc.scalar.activation(g_out[:, cols(b)], ps[:, 6 + b % 2, :], ACT.Silu).then_inc(down_copied, 1)

            for n, (b, c) in enumerate(units):
                act.wait_ge(expert_product, n + 1)
                if n >= 4:
                    act.wait_ge(down_product, n - 3)
                nc.scalar.activation(acts[n % 4], ps[:, 3 * (n % 2), :], ACT.Silu).then_inc(silu_done, 1)
                if b >= 1 and c == 2:
                    store(b - 1)
            store(BATCH - 1)

        @block.vector
        def _(dve):
            for n in range(len(units)):
                dve.wait_ge(silu_done, n + 1)
                bank = 3 * (n % 2)
                nc.vector.tensor_tensor(acts[n % 4], acts[n % 4], ps[:, bank + 1, :], ALU.mult).then_inc(act_step, 1)
                dve.wait_ge(act_step, n + 1)
                nc.vector.tensor_tensor(acts[n % 4], acts[n % 4], ps[:, bank + 2, :], ALU.mult).then_inc(act_ready, 1)


def rank_before(link, v, rank, value, cmp, n):
    for d in range(1, n):
        lo, hi = slice(0, n - d), slice(d, n)
        link(v.tensor_tensor(cmp[:, :, lo], value[:, :, lo], value[:, :, hi], ALU.is_ge))
        link(v.tensor_tensor(rank[:, :, hi], rank[:, :, hi], cmp[:, :, lo], ALU.add))
        link(v.tensor_tensor(cmp[:, :, lo], value[:, :, lo], value[:, :, hi], ALU.is_lt))
        link(v.tensor_tensor(rank[:, :, lo], rank[:, :, lo], cmp[:, :, lo], ALU.add))


def columns_of(W, parts):
    where, _ = offsets(parts)

    def w(name, a=0, n=None, rows=slice(0, P)):
        o, width = where[name]
        return W[rows, o + a:o + (a + n if n else width)]
    return w


def block2(nc, m, ins, x):
    xn, g, s = m.slab(1), m.slab(2), m.slab(3)
    WA = m.slab(4)[:, 0:offsets(A_PARTS)[1]]
    WM = m.weights[:, 0:offsets(M_PARTS)[1]]
    load(nc, [(WA, ins["A2"]), (WM, ins["M2"])], "l2")
    layer_norm(nc, m, x, xn, tag="l2ln")
    wa, wm = columns_of(WA, A_PARTS), columns_of(WM, M_PARTS)
    weights = {"q": lambda c: wa("q2", c * P, P), "k": lambda c: wa("k2", c * P, P), "v": wa("v2"), "o": wa("o2"),
               "v_row": wa("v_row2", rows=slice(0, 1)), "bq": lambda c: wa("bq2", c, 1), "bk": lambda c: wa("bk2", c, 1),
               "bo": wa("bo2")}
    experts(nc, m, wm, xn, g)
    full_attention(nc, m, xn, s, weights, 16, 8 ** -0.5, True)
    add_product(nc, x, s, g)


RETAIN_LAYERS = 4
S_PARTS = [("k", P), ("q", P), ("v", P), ("m1", 2 * P), ("m2", P), ("f1", 2 * P), ("f2", 2 * P), ("bm1", 2), ("bm2", 1),
           ("gn_g", 1), ("gn_b", 1), ("bf1", 2), ("bf2", 1), ("ln_g", 1), ("ln_b", 1)]
N_PARTS = [("q3", 2 * P), ("k3", 2 * P), ("v3", P), ("o3", P), ("v_row3", P), ("bq3", 2), ("bk3", 2), ("bo3", 1),
           ("norm_w", 1), ("norm_b", 1)]


def retention_network(nc, m, ins, xn, s_out):
    W = m.weights[:, 0:offsets(S_PARTS)[1]]
    w = columns_of(W, S_PARTS)
    h, r = m.slab(3), m.slab(4)
    falloff = m.slab(5).rearrange("p (t k) -> p t k", t=4)
    with phase(nc, "falloff_loaded") as (block, falloff_loaded):
        @block.sync
        def _(sp):
            sp.dma_start(m.slab(5), ins["falloff"]).then_inc(falloff_loaded, 16)
            sp.wait_ge(falloff_loaded, 16)

        @block.vector
        def _(dve):
            nc.vector.tensor_copy(h, xn)

    with nc.Fori(0, RETAIN_LAYERS) as layer:
        load(nc, [(W, ins["S3"][bass.ds(layer, 1)].rearrange("l p n -> (l p) n"))], "retention_layer")
        with nc.Fori(0, BATCH) as batch:
            retention(nc, m, w, falloff, h, r, batch)
        retention_feed_forward(nc, m, w, r, h)
        layer_norm(nc, m, r, h, w("ln_g"), w("ln_b"), tag="ret")
    with phase(nc, "copied_out") as (block, copied_out):
        @block.vector
        def _(dve):
            nc.vector.tensor_copy(s_out, h)


def retention(nc, m, w, falloff, h, r, batch):
    ps = m.psum
    hb, k, q = (m.slab(6)[:, 512 * i:512 * i + 512] for i in range(3))
    v = m.slab(7)[:, 0:512].rearrange("p (t d) -> p t d", t=4)
    kept = [m.slab(8)[:, 512 * n:512 * n + 512] for n in range(4)]
    keptT = [m.slab(9)[:, 512 * n:512 * n + 512].rearrange("p (k q) -> p k q", k=4) for n in range(4)]
    sums = m.slab(7)[:, 512:544]
    with phase(nc, "h_staged qk_product qk_done v_product v_done score_product decayed denom_ready divided "
                   "turned turned_copied r_product r_copied denom_step") as (
            block, h_staged, qk_product, qk_done, v_product, v_done, score_product, decayed, denom_ready, divided,
            turned, turned_copied, r_product, r_copied, denom_step):
        @block.tensor
        def _(pe):
            pe.wait_ge(h_staged, 1)
            nc.tensor.matmul(ps[:, 0, :], w("k"), hb, start=True, stop=True).then_inc(qk_product, 1)
            nc.tensor.matmul(ps[:, 1, :], w("q"), hb, start=True, stop=True).then_inc(qk_product, 1)
            for t in range(4):
                last = nc.tensor.matmul(ps[:, 2, t * P:t * P + P], hb[:, t * P:t * P + P], w("v"), start=True, stop=True)
            last.then_inc(v_product, 1)
            pe.wait_ge(qk_done, 2)
            for t in range(4):
                n = (t + 1) * P
                nc.tensor.matmul(ps[:, 4 + t, 0:n], q[:, t * P:t * P + P], k[:, 0:n], start=True, stop=True).then_inc(score_product, 1)
            pe.wait_ge(v_done, 1)
            for t in range(4):
                pe.wait_ge(divided, t + 1)
                for c in range(t + 1):
                    last = nc.tensor.transpose(ps[:, t, c * P:c * P + P], kept[t][:, c * P:c * P + P], m.ident)
                last.then_inc(turned, 1)
            for t in range(4):
                pe.wait_ge(turned_copied, t + 1)
                for c in range(t + 1):
                    last = nc.tensor.matmul(ps[:, 4 + t, 0:P], v[:, c, :], keptT[t][:, c, :], start=(c == 0), stop=(c == t))
                last.then_inc(r_product, 1)

        def copy_turned(act, t):
            act.wait_ge(turned, t + 1)
            nc.scalar.activation(keptT[t][:, 0:t + 1, :], ps[:, t, 0:(t + 1) * P].rearrange("p (k q) -> p k q", q=P),
                                 ACT.Copy).then_inc(turned_copied, 1)

        @block.scalar
        def _(act):
            nc.scalar.activation(hb, h[:, bass.ds(batch * SEQ, SEQ)], ACT.Copy).then_inc(h_staged, 1)
            for i, dst in enumerate((k, q)):
                act.wait_ge(qk_product, i + 1)
                nc.scalar.activation(dst, ps[:, i, :], ACT.Copy).then_inc(qk_done, 1)
            act.wait_ge(v_product, 1)
            nc.scalar.activation(v, ps[:, 2, :].rearrange("p (t d) -> p t d", t=4), ACT.Copy).then_inc(v_done, 1)
            for t in range(4):
                n = (t + 1) * P
                act.wait_ge(denom_ready, t + 1)
                nc.scalar.activation(kept[t][:, 0:n], kept[t][:, 0:n], ACT.Copy, scale=sums[:, 8 * t + 2:8 * t + 3]).then_inc(divided, 1)
                if t >= 1:
                    copy_turned(act, t - 1)
            copy_turned(act, 3)

        @block.vector
        def _(dve):
            link = Chain(dve, denom_step)
            for t in range(4):
                n = (t + 1) * P
                dve.wait_ge(score_product, t + 1)
                a = sums[:, 8 * t:8 * t + 8]
                link(nc.vector.tensor_tensor_reduce(kept[t][:, 0:n], ps[:, 4 + t, 0:n], falloff[:, t, 0:n], 1.0, 0.0,
                                                    ALU.mult, ALU.add, a[:, 0:1]))
                link(nc.vector.tensor_scalar(a[:, 1:2], a[:, 0:1], -1.0, None, ALU.mult))
                link(nc.vector.tensor_tensor(a[:, 0:1], a[:, 0:1], a[:, 1:2], ALU.max))
                link(nc.vector.tensor_scalar(a[:, 1:2], a[:, 0:1], 1.0, None, ALU.max))
                nc.vector.reciprocal(a[:, 2:3], a[:, 1:2]).then_inc(denom_ready, 1)
            for t in range(4):
                dve.wait_ge(r_product, t + 1)
                nc.vector.tensor_copy(r[:, bass.ds(batch * SEQ + t * P, P)], ps[:, 4 + t, 0:P]).then_inc(r_copied, 1)


def retention_feed_forward(nc, m, w, r, h):
    ps = m.psum
    a, y = m.slab(6), m.slab(7)
    stats = m.slab(8)[:, 0:64]
    junk = m.slab(9)
    with phase(nc, "m1_product silu_done a_ready m2_product m2_done sum_product centred squared square_product std_ready "
                   "scale_ready normed y_ready mean_step") as (
            block, m1_product, silu_done, a_ready, m2_product, m2_done, sum_product, centred, squared, square_product, std_ready,
            scale_ready, normed, y_ready, mean_step):
        @block.tensor
        def _(pe):
            for b in range(BATCH):
                nc.tensor.matmul(ps[:, 2 * b + 1, :], w("m1", P, P), r[:, cols(b)], start=True, stop=True)
                nc.tensor.matmul(ps[:, 2 * b, :], w("m1", 0, P), r[:, cols(b)], start=True, stop=True).then_inc(m1_product, 1)
            for b in range(BATCH):
                pe.wait_ge(a_ready, b + 1)
                nc.tensor.matmul(ps[:, 2 * b, :], w("m2"), a[:, cols(b)], start=True, stop=True).then_inc(m2_product, 1)
            pe.wait_ge(m2_done, 4)
            nc.tensor.matmul(ps[:, 1, 0:BATCH], m.mean, stats[:, 0:BATCH], start=True, stop=True).then_inc(sum_product, 1)
            pe.wait_ge(squared, 4)
            nc.tensor.matmul(ps[:, 3, 0:BATCH], m.mean, stats[:, 8:8 + BATCH], start=True, stop=True).then_inc(square_product, 1)

        @block.scalar
        def _(act):
            for b in range(BATCH):
                act.wait_ge(m1_product, b + 1)
                nc.scalar.activation(a[:, cols(b)], ps[:, 2 * b + 1, :], ACT.Silu, bias=w("bm1", 1, 1)).then_inc(silu_done, 1)
            for b in range(BATCH):
                act.wait_ge(m2_product, b + 1)
                nc.scalar.activation(y[:, cols(b)], ps[:, 2 * b, :], ACT.Identity, bias=w("bm2"),
                                     accum_out=stats[:, b:b + 1]).then_inc(m2_done, 1)
            for b in range(BATCH):
                act.wait_ge(centred, b + 1)
                nc.scalar.activation(junk[:, cols(b)], y[:, cols(b)], ACT.Square,
                                     accum_out=stats[:, 8 + b:9 + b]).then_inc(squared, 1)
            act.wait_ge(square_product, 1)
            nc.scalar.activation(stats[:, 16:16 + BATCH], ps[:, 3, 0:BATCH], ACT.Sqrt, scale=1.0 / SEQ,
                                 bias=m.tiny[:, 0:1]).then_inc(std_ready, 1)
            for b in range(BATCH):
                act.wait_ge(scale_ready, 1)
                nc.scalar.activation(y[:, cols(b)], y[:, cols(b)], ACT.Identity, bias=w("gn_b"),
                                     scale=stats[:, 24 + b:25 + b]).then_inc(normed, 1)

        @block.vector
        def _(dve):
            for b in range(BATCH):
                dve.wait_ge(silu_done, b + 1)
                nc.vector.scalar_tensor_tensor(out=a[:, cols(b)], in0=ps[:, 2 * b, :], scalar=w("bm1", 0, 1), in1=a[:, cols(b)],
                                               op0=ALU.add, op1=ALU.mult).then_inc(a_ready, 1)
            dve.wait_ge(sum_product, 1)
            link = Chain(dve, mean_step)
            link(nc.vector.tensor_scalar(stats[:, 32:32 + BATCH], ps[:, 1, 0:BATCH], 1.0 / SEQ, None, ALU.mult))
            for b in range(BATCH):
                nc.vector.tensor_scalar(y[:, cols(b)], y[:, cols(b)], stats[:, 32 + b:33 + b], None, ALU.subtract).then_inc(centred, 1)
            dve.wait_ge(std_ready, 1)
            link(nc.vector.reciprocal(stats[:, 16:16 + BATCH], stats[:, 16:16 + BATCH]))
            nc.vector.tensor_scalar(stats[:, 24:24 + BATCH], stats[:, 16:16 + BATCH], w("gn_g"), None, ALU.mult).then_inc(scale_ready, 1)
            for b in range(BATCH):
                dve.wait_ge(normed, b + 1)
                nc.vector.tensor_tensor(y[:, cols(b)], y[:, cols(b)], h[:, cols(b)], ALU.add).then_inc(y_ready, 1)

    hidden = [m.slab(8), m.slab(9)]
    units = [(b, c) for b in range(BATCH) for c in range(2)]
    with phase(nc, "f1_product gelu_done f2_product") as (block, f1_product, gelu_done, f2_product):
        @block.tensor
        def _(pe):
            for n, (b, c) in enumerate(units):
                if n >= 4:
                    pe.wait_ge(gelu_done, n - 3)
                nc.tensor.matmul(ps[:, n % 4, :], w("f1", c * P, P), y[:, cols(b)], start=True, stop=True).then_inc(f1_product, 1)
            for b in range(BATCH):
                pe.wait_ge(gelu_done, 2 * b + 2)
                nc.tensor.matmul(ps[:, 4 + b, :], w("f2", 0, P), hidden[0][:, cols(b)], start=True, stop=False)
                nc.tensor.matmul(ps[:, 4 + b, :], w("f2", P, P), hidden[1][:, cols(b)], start=False, stop=True).then_inc(f2_product, 1)

        @block.scalar
        def _(act):
            for n, (b, c) in enumerate(units):
                act.wait_ge(f1_product, n + 1)
                nc.scalar.activation(hidden[c][:, cols(b)], ps[:, n % 4, :], ACT.Gelu, bias=w("bf1", c, 1)).then_inc(gelu_done, 1)

        @block.vector
        def _(dve):
            for b in range(BATCH):
                dve.wait_ge(f2_product, b + 1)
                nc.vector.scalar_tensor_tensor(out=r[:, cols(b)], in0=ps[:, 4 + b, :], scalar=w("bf2"), in1=y[:, cols(b)],
                                               op0=ALU.add, op1=ALU.add)


def nested_attention(nc, m, ins, xn, g_out):
    W = m.slab(3)[:, 0:offsets(N_PARTS)[1]]
    w = columns_of(W, N_PARTS)
    nested, normed = m.slab(4)[:, 0:SEQ], m.slab(5)
    load(nc, [(W, ins["N3"]), (nested, ins["nested"])], "nested")
    layer_norm(nc, m, xn, normed, w("norm_w"), w("norm_b"), tag="nested_norm")
    with phase(nc, "narrowed") as (block, narrowed):
        @block.vector
        def _(dve):
            for b in range(BATCH):
                nc.vector.tensor_tensor(normed[:, cols(b)], normed[:, cols(b)], nested, ALU.mult)
    weights = {"q": lambda c: w("q3", c * P, P), "k": lambda c: w("k3", c * P, P), "v": w("v3"), "o": w("o3"),
               "v_row": w("v_row3", rows=slice(0, 1)), "bq": lambda c: w("bq3", c, 1), "bk": lambda c: w("bk3", c, 1),
               "bo": w("bo3")}
    full_attention(nc, m, normed, g_out, weights, 8, P ** -0.5, False, mask=nested)
    with phase(nc, "x_added") as (block, x_added):
        @block.vector
        def _(dve):
            for b in range(BATCH):
                nc.vector.tensor_tensor(g_out[:, cols(b)], g_out[:, cols(b)], xn[:, cols(b)], ALU.add).then_inc(x_added, 1)

        @block.scalar
        def _(act):
            for b in range(BATCH):
                act.wait_ge(x_added, b + 1)
                nc.scalar.activation(g_out[:, cols(b)], g_out[:, cols(b)], ACT.Silu)


def block3(nc, m, ins, x):
    xn, g, s = m.slab(1), m.slab(2), m.slab(4)
    layer_norm(nc, m, x, xn, tag="l3ln")
    nested_attention(nc, m, ins, xn, g)
    retention_network(nc, m, ins, xn, s)
    add_product(nc, x, s, g)


def block1(nc, m, ins, x):
    xn = m.slab(1)
    layer_norm(nc, m, x, xn, tag="l1ln", refine=False)
    g, s = m.slab(2), m.slab(4)
    local_transformer(nc, m, ins, xn, g)
    recurrent_network(nc, m, ins, xn, s)
    add_product(nc, x, s, g)


BLOCKS = [block0, block1, block2, block3]


def build_program(nc, ins, out, blocks=(0, 1, 2, 3)):
    with ExitStack() as ctx:
        m = Memory(nc, ctx)
        x = m.slab(0)
        load(nc, [(x, ins["x"]), (m.const[:, :], ins["const"])], "x")
        for i in blocks:
            BLOCKS[i](nc, m, ins, x)
        with phase(nc, "stored") as (block, stored):
            @block.sync
            def _(sp):
                sp.dma_start(out, x).then_inc(stored, 16)
                sp.wait_ge(stored, 16)


def pack(parts, arrays):
    where, width = offsets(parts)
    out = np.zeros((P, width), np.float32)
    for name, a in arrays.items():
        at, w = where[name]
        assert a.shape[1] == w, (name, a.shape, w)
        out[:a.shape[0], at:at + w] = a
    return out


def chunk_cols(v, n):
    return v.reshape(n, -1).T


def constants():
    block = np.kron(np.eye(2), np.ones((64, 64)))
    tiny = np.zeros((P, 4))
    tiny[:, 0] = LN_EPS
    tiny[:, 1] = 1e-6
    return pack(CONST_PARTS, {
        "mean": np.full((P, P), 1.0 / P), "ident": np.eye(P), "halves": block, "mean_halves": block / 64, "tiny": tiny, "ones_row": np.ones((1, P))})


def rotary_tables():
    f = np.float32
    half = np.arange(0, HD1, 2, dtype=f)
    inv_freq = (f(1.0) / f(10000.0) ** (half / f(HD1))).astype(f)
    t = np.arange(SEQ, dtype=f)
    freqs = np.concatenate([t[:, None] * inv_freq[None, :]] * 2, -1)
    base = (half + f(0.4 * HD1)) / f(1.4 * HD1)
    scale = base[None, :] ** ((t - SEQ // 2) / f(REACH // 2))[:, None]
    scale = np.concatenate([scale, scale], -1).astype(f)
    sign = np.where(np.arange(HD1) < HD1 // 2, f(-1), f(1))
    inv = f(1.0) / scale
    cos, sin = np.cos(freqs), np.sin(freqs) * sign
    return np.concatenate([np.tile(a.T, (2, 1)) for a in (cos * scale, sin * scale, cos * inv, sin * inv)], 1).astype(f)


def window_masks():
    q, k = np.arange(P)[:, None], np.arange(REACH + P)[None, :] - REACH
    seen = (q >= k) & (q - k <= REACH)
    return np.concatenate([np.where(s, 0, MASKED) for s in (seen & (k >= 0), seen)], 1).astype(np.float32)


def pad_cols(a, n):
    return np.concatenate([a, np.zeros((a.shape[0], n - a.shape[1]), a.dtype)], 1)


def local_layer(i, n):
    inner = HEADS1 * HD1
    turn = (np.arange(inner).reshape(HEADS1, 2, HD1 // 2)[:, ::-1]).reshape(-1)
    wq, wk, wv = (i["L1_ffn_Wqkv"][n][:, c * inner:(c + 1) * inner] for c in range(3))
    qk = np.stack([a.reshape(P, 8, P) for a in (wq, wq[:, turn], wk, wk[:, turn])], 2).reshape(P, -1)
    qs, ks, half = i["L1_ffn_q_scale"][n], i["L1_ffn_k_scale"][n], turn[:HD1]
    up = i["L1_ffn_W1"][n]
    b_up = i["L1_ffn_b1"][n]
    chunks = [slice(h * FF1 + c * P, h * FF1 + min((c + 1) * P, FF1)) for h in range(2) for c in range(3)]
    return pack(F1_PARTS, {
        "qk": qk, "v": wv, "out": i["L1_ffn_Wo"][n].reshape(8, P, P).transpose(1, 0, 2).reshape(P, -1),
        "up": np.concatenate([pad_cols(up[:, c], P) for c in chunks], 1),
        "down": np.concatenate([np.pad(i["L1_ffn_W2"][n][c], ((0, P - (c.stop - c.start)), (0, 0))) for c in chunks[:3]], 1),
        "scales": np.stack([np.tile(a, 2) for a in (qs, qs[half], ks, ks[half])], 1),
        "ln_g": i["L1_ffn_ln_g"][n][:, None], "ln_b": i["L1_ffn_ln_b"][n][:, None],
        "b_up": np.stack([np.pad(b_up[c], (0, P - (c.stop - c.start))) for c in chunks], 1),
        "b_down": i["L1_ffn_b2"][n][:, None]})


def spread_table():
    out = np.zeros((P, 192), np.float32)
    out[:64, 63] = 1
    out[64:, 127] = 1
    return out


def recurrent_layer(i, n):
    a = {name: i[f"L1_attn_{name}"][n] for name in (
        "tm_w1", "td_w1", "td_w2", "Wr", "Wk", "Wv", "Wg", "Wo", "cWk", "cWr")}
    for name in ("ln1_w", "ln2_w", "x_maa", "w_maa", "k_maa", "v_maa", "r_maa", "g_maa", "gn_w", "gn_b", "ck_maa", "cr_maa"):
        a[name] = i[f"L1_attn_{name}"][n][:, None]
    for name in ("time_decay", "time_first"):
        a[name] = i[f"L1_attn_{name}"][n].reshape(P, 1)
    tm = i["L1_attn_tm_w2"][n]
    a["tm_w2"], a["tm_w2_last"] = tm[:4].reshape(4 * MIX, P), tm[4]
    a["cWv"] = i["L1_attn_cWv"][n].reshape(3, P, P).transpose(1, 0, 2).reshape(P, -1)
    a["ln_out_w"] = i["L1_attn_ln_out_w"][:, None]
    return pack(R_PARTS, a)


def spread_heads(a, heads):
    out = np.zeros((a.shape[0], heads, 32), a.dtype)
    out[:, :, :P // heads] = a.reshape(-1, heads, P // heads)
    return out.reshape(a.shape[0], -1)


def attention_pack(i):
    p = "L2_attn_"
    return pack(A_PARTS, {
        "q2": spread_heads(i[p + "Wq"].T, 16), "k2": spread_heads(i[p + "Wk"].T, 16), "v2": i[p + "Wv"].T, "o2": i[p + "Wo"].T,
        "v_row2": i[p + "bv"][None], "bq2": chunk_cols(spread_heads(i[p + "bq"][None], 16), 4),
        "bk2": chunk_cols(spread_heads(i[p + "bk"][None], 16), 4), "bo2": i[p + "bo"][:, None]})


def expert_pack(i):
    p = "L2_ffn_"
    rows = np.kron(np.eye(EXPERTS), np.ones((1, 64)))
    down = i[p + "down_proj"].transpose(0, 2, 1).reshape(8, P, P).transpose(1, 0, 2).reshape(P, -1)
    return pack(M_PARTS, {
        "router": i[p + "gate_weight"].T, "gate": i[p + "gate_proj"].reshape(-1, P).T, "up": i[p + "up_proj"].reshape(-1, P).T,
        "down": down, "rows": rows, "e_bias": np.tile(i[p + "e_bias"][None], (P, TOK // P))})


def retention_falloff():
    q, k = np.arange(SEQ)[:, None], np.arange(SEQ)[None, :]
    a = (q >= k) / (1.0 + np.sqrt(q)) / np.sqrt(P)
    return a.reshape(4, P, SEQ).transpose(1, 0, 2).reshape(P, -1).astype(np.float32)


def retention_pack(i, n):
    a = {name: i["L3_attn_" + name][n] for name in ("Wkqv", "Wm1", "Wm2", "Wf1", "Wf2", "bm1", "bm2", "gn_g", "gn_b", "bf1",
                                                    "bf2", "ln_g", "ln_b")}
    k, q, v = (a["Wkqv"][:, c * P:(c + 1) * P] for c in range(3))
    return pack(S_PARTS, {
        "k": k, "q": q, "v": v, "m1": a["Wm1"], "m2": a["Wm2"], "f1": a["Wf1"],
        "f2": a["Wf2"].reshape(2, P, P).transpose(1, 0, 2).reshape(P, -1), "bm1": chunk_cols(a["bm1"], 2),
        "bf1": chunk_cols(a["bf1"], 2), **{name: a[name][:, None] for name in ("bm2", "gn_g", "gn_b", "bf2", "ln_g", "ln_b")}})


def nested_mask():
    return (np.arange(P)[:, None] < (P >> (np.arange(SEQ) // P))[None, :]).astype(np.float32)


def nested_pack(i):
    p = "L3_ffn_"
    return pack(N_PARTS, {
        "q3": spread_heads(i[p + "q_w"].T, 8), "k3": spread_heads(i[p + "k_w"].T, 8), "v3": i[p + "v_w"].T, "o3": i[p + "o_w"].T,
        "v_row3": i[p + "v_b"][None], "bq3": chunk_cols(spread_heads(i[p + "q_b"][None], 8), 2),
        "bk3": chunk_cols(spread_heads(i[p + "k_b"][None], 8), 2), "bo3": i[p + "o_b"][:, None],
        "norm_w": i[p + "norm_w"][:, None], "norm_b": i[p + "norm_b"][:, None]})


def lay_out(i):
    h = HID
    arrays = {"x": i["L0_attn_x"].reshape(TOK, P).T, "const": constants()}
    conv_w = np.concatenate([i["L0_attn_conv_w"][:HC], i["L0_attn_conv_w"][HC:]], axis=1)
    arrays["L0"] = pack(L0_PARTS, {
        "w_gate": i["L0_attn_W_in"][:h].T, "w_x": i["L0_attn_W_in"][h:].T,
        "w_gates0": i["L0_attn_W_gates"].T[:HC], "w_gates1": i["L0_attn_W_gates"].T[HC:],
        "w_out0": i["L0_attn_W_out"].T[:HC], "w_out1": i["L0_attn_W_out"].T[HC:],
        "ffn": i["L0_ffn_weight"].T, "disha": np.concatenate([i["L0_ffn_disha"]] * 2),
        "conv_w": conv_w, "conv_b": chunk_cols(i["L0_attn_conv_b"], 2),
        "b_forget": chunk_cols(i["L0_attn_b_gates"][:h], 2), "b_inp": chunk_cols(i["L0_attn_b_gates"][h:], 2),
        "forget_base": chunk_cols(i["L0_attn_forget_base"], 2)})
    arrays["rotary"], arrays["masks"] = rotary_tables(), window_masks()
    arrays["spread"] = spread_table()
    arrays["R"] = np.stack([recurrent_layer(i, n) for n in range(2)])
    arrays["A2"], arrays["M2"] = attention_pack(i), expert_pack(i)
    arrays["S3"] = np.stack([retention_pack(i, n) for n in range(RETAIN_LAYERS)])
    arrays["N3"], arrays["nested"], arrays["falloff"] = nested_pack(i), nested_mask(), retention_falloff()
    arrays["F1"] = np.stack([local_layer(i, n) for n in range(6)])
    return {k: np.ascontiguousarray(v) for k, v in arrays.items()}


def kernel(**inputs):
    import concourse.bacc as bacc
    from concourse.bass_utils import run_bass_kernel_spmd

    arrays = lay_out({k: np.asarray(v) for k, v in inputs.items()})
    nc = bacc.Bacc("TRN2", target_bir_lowering=False, num_devices=1)
    ins = {k: nc.dram_tensor(k, v.shape, F32, kind="ExternalInput").ap() for k, v in arrays.items()}
    out = nc.dram_tensor("out", (P, TOK), F32, kind="ExternalOutput").ap()
    build_program(nc, ins, out)
    r = run_bass_kernel_spmd(nc, [arrays], core_ids=[0])
    return np.ascontiguousarray(r.results[0]["out"].T).reshape(BATCH, SEQ, P)
```
